# Optimizing a Trainium2 kernel written in Bass

```python
import numpy as np
import jax
import jax.numpy as jnp

def _softmax(x, axis=-1):
    return jax.nn.softmax(x, axis=axis)

def _gelu(x):
    return jax.nn.gelu(x, approximate=True)

def _silu(x):
    return jax.nn.silu(x)

def _sigmoid(x):
    return jax.nn.sigmoid(x)

def _layernorm(x, axis=-1, eps=1e-05):
    m = jnp.mean(x, axis=axis, keepdims=True)
    v = jnp.var(x, axis=axis, keepdims=True)
    return (x - m) / jnp.sqrt(v + eps)

def _scatter_add(tgt, idx, src, axis=0):
    return tgt.at[idx].add(src)

def _segment_sum(src, seg, n):
    return jax.ops.segment_sum(src, seg, n)
kernel_name = 'mk_hybrid_d2_jaxref_r8_adaa50'

def setup_inputs(seed: int=0):
    np.random.seed(seed)
    _w = jnp.asarray

    def _L0_attn_a_setup():
        import jax, jax.numpy as jnp
        import numpy as np
        key = jax.random.key(seed)
        x = jax.random.normal(key, (8, 512, 128), dtype=jnp.float32)
        return {'x': x}
    _L0_attn_a_in = _L0_attn_a_setup()

    def _L0_attn_b_setup():
        import jax, jax.numpy as jnp
        import numpy as np
        from math import sqrt
        EMBED = 128
        HEADS = 16
        key = jax.random.key(seed)
        k1, k2, k3, k4, k5 = jax.random.split(key, 5)
        x = jax.random.normal(k1, (2, 256, EMBED), dtype=jnp.float32)
        s = 1.0 / sqrt(EMBED)
        W_qkv = jax.random.normal(k2, (EMBED, 3 * EMBED), dtype=jnp.float32) * s
        b_qkv = jax.random.normal(k3, (3 * EMBED,), dtype=jnp.float32) * 0.01
        W_out = jax.random.normal(k4, (EMBED, EMBED), dtype=jnp.float32) * s
        b_out = jax.random.normal(k5, (EMBED,), dtype=jnp.float32) * 0.01
        return {'x': x, 'W_qkv': W_qkv, 'b_qkv': b_qkv, 'W_out': W_out, 'b_out': b_out}
    _L0_attn_b_in = _L0_attn_b_setup()

    def _L0_ffn_setup():
        import jax, jax.numpy as jnp
        import numpy as np
        E, D, DFF = (8, 128, 512)
        key = jax.random.key(seed)
        ks = jax.random.split(key, 10)
        s = 0.02
        return {'x': jax.random.normal(ks[0], (4, 256, D), dtype=jnp.float32), 'Wr': jax.random.normal(ks[1], (D, E), dtype=jnp.float32) * s, 'br': jnp.zeros((E,), dtype=jnp.float32), 'W1': jax.random.normal(ks[2], (E, D, DFF), dtype=jnp.float32) * s, 'b1': jnp.zeros((E, DFF), dtype=jnp.float32), 'W2': jax.random.normal(ks[3], (E, D, DFF), dtype=jnp.float32) * s, 'b2': jnp.zeros((E, DFF), dtype=jnp.float32), 'W3': jax.random.normal(ks[4], (E, DFF, D), dtype=jnp.float32) * s, 'b3': jnp.zeros((E, D), dtype=jnp.float32)}
    _L0_ffn_in = _L0_ffn_setup()

    def _L1_attn_a_setup():
        import jax, jax.numpy as jnp
        import numpy as np
        BASE_FREQUENCY = 10000.0
        LRP = 17
        MIN_L = 1.0 - LRP / 100.0
        SDT_L = (BASE_FREQUENCY - MIN_L * BASE_FREQUENCY) * 2.0
        ARM_ATTENTION = 2.0
        HEADS_DIM = 64

        def _nrope(xs, base, angle_range):
            N, T, d = xs.shape
            half = d // 2
            inv_freq = base ** (-jnp.arange(half, dtype=jnp.float32) / half)
            pos = jnp.arange(T, dtype=jnp.float32)
            scale = angle_range / jnp.maximum(T - 1, 1)
            ang = pos[:, None] * inv_freq[None, :] * scale
            cos, sin = (jnp.cos(ang), jnp.sin(ang))
            x1, x2 = (xs[..., :half], xs[..., half:])
            return jnp.concatenate([x1 * cos - x2 * sin, x1 * sin + x2 * cos], axis=-1)
        key = jax.random.key(seed)
        ks = jax.random.split(key, 9)
        B, T, E = (4, 128, 128)
        x = jax.random.normal(ks[0], (B, T, E), dtype=jnp.float32)

        def w(k):
            return jax.random.normal(k, (E, E), dtype=jnp.float32) * 0.02
        z = jnp.zeros((E,), dtype=jnp.float32)
        return {'x': x, 'Wq': w(ks[1]), 'bq': z, 'Wk': w(ks[2]), 'bk': z, 'Wv': w(ks[3]), 'bv': z, 'Wo': w(ks[4]), 'bo': z, 'nrope_freq': jnp.zeros((1,), dtype=jnp.float32)}
    _L1_attn_a_in = _L1_attn_a_setup()

    def _L1_attn_b_setup():
        import jax, jax.numpy as jnp
        import numpy as np
        N_HEAD = 16
        WINDOW = 128
        CAUSAL = False

        def _window_attention(x, w_in, b_in, w_out, b_out):
            B, T, D = x.shape
            H = N_HEAD
            hd = D // H
            scale = 1.0 / jnp.sqrt(jnp.float32(hd))
            qkv = jnp.einsum('btd,ed->bte', x, w_in) + b_in
            q, k, v = jnp.split(qkv, 3, axis=-1)
            q = q.reshape(B, T, H, hd).transpose(0, 2, 1, 3)
            k = k.reshape(B, T, H, hd).transpose(0, 2, 1, 3)
            v = v.reshape(B, T, H, hd).transpose(0, 2, 1, 3)
            scores = jnp.einsum('bhqd,bhkd->bhqk', q, k) * scale
            idx = jnp.arange(T)
            diff = idx[:, None] - idx[None, :]
            if CAUSAL:
                allowed = (diff >= 0) & (diff <= WINDOW)
            else:
                allowed = jnp.abs(diff) <= WINDOW
            NEG = jnp.float32(-1e+30)
            scores = jnp.where(allowed[None, None, :, :], scores, NEG)
            attn = jax.nn.softmax(scores, axis=-1)
            ctx = jnp.einsum('bhqk,bhkd->bhqd', attn, v)
            ctx = ctx.transpose(0, 2, 1, 3).reshape(B, T, D)
            out = jnp.einsum('btd,ed->bte', ctx, w_out) + b_out
            return x + out
        key = jax.random.key(seed)
        ks = jax.random.split(key, 5)
        B, T, D = (1, 512, 128)
        x = jax.random.normal(ks[0], (B, T, D), dtype=jnp.float32)
        w_in = jax.random.normal(ks[1], (3 * D, D), dtype=jnp.float32) * 0.02
        b_in = jax.random.normal(ks[2], (3 * D,), dtype=jnp.float32) * 0.02
        w_out = jax.random.normal(ks[3], (D, D), dtype=jnp.float32) * 0.02
        b_out = jax.random.normal(ks[4], (D,), dtype=jnp.float32) * 0.02
        return {'x': x, 'w_in': w_in, 'b_in': b_in, 'w_out': w_out, 'b_out': b_out}
    _L1_attn_b_in = _L1_attn_b_setup()

    def _L1_ffn_setup():
        import jax, jax.numpy as jnp
        import numpy as np
        B, S, H, E, K = (2, 128, 128, 8, 2)
        F = 4 * H
        key = jax.random.key(seed)
        ks = jax.random.split(key, 8)
        std = 0.02
        return {'x': jax.random.normal(ks[0], (B, S, H), jnp.float32), 'gate_w': jax.random.normal(ks[1], (E, H), jnp.float32) * (std / np.sqrt(H)), 'gate_bias': jnp.zeros((E,), jnp.float32), 'Wu': jax.random.normal(ks[2], (E, F, H), jnp.float32) * std, 'bu': jnp.zeros((E, F), jnp.float32), 'Wd': jax.random.normal(ks[3], (E, H, F), jnp.float32) * std, 'bd': jnp.zeros((E, H), jnp.float32), 'sWu': jax.random.normal(ks[4], (F, H), jnp.float32) * std, 'sbu': jnp.zeros((F,), jnp.float32), 'sWd': jax.random.normal(ks[5], (H, F), jnp.float32) * std, 'sbd': jnp.zeros((H,), jnp.float32)}
    _L1_ffn_in = _L1_ffn_setup()
    _d = {'L0_attn_a_x': _L0_attn_a_in['x'], 'L0_attn_b_W_qkv': _L0_attn_b_in['W_qkv'], 'L0_attn_b_b_qkv': _L0_attn_b_in['b_qkv'], 'L0_attn_b_W_out': _L0_attn_b_in['W_out'], 'L0_attn_b_b_out': _L0_attn_b_in['b_out'], 'L0_ffn_Wr': _L0_ffn_in['Wr'], 'L0_ffn_br': _L0_ffn_in['br'], 'L0_ffn_W1': _L0_ffn_in['W1'], 'L0_ffn_b1': _L0_ffn_in['b1'], 'L0_ffn_W2': _L0_ffn_in['W2'], 'L0_ffn_b2': _L0_ffn_in['b2'], 'L0_ffn_W3': _L0_ffn_in['W3'], 'L0_ffn_b3': _L0_ffn_in['b3'], 'L1_attn_a_Wq': _L1_attn_a_in['Wq'], 'L1_attn_a_bq': _L1_attn_a_in['bq'], 'L1_attn_a_Wk': _L1_attn_a_in['Wk'], 'L1_attn_a_bk': _L1_attn_a_in['bk'], 'L1_attn_a_Wv': _L1_attn_a_in['Wv'], 'L1_attn_a_bv': _L1_attn_a_in['bv'], 'L1_attn_a_Wo': _L1_attn_a_in['Wo'], 'L1_attn_a_bo': _L1_attn_a_in['bo'], 'L1_attn_a_nrope_freq': _L1_attn_a_in['nrope_freq'], 'L1_attn_b_w_in': _L1_attn_b_in['w_in'], 'L1_attn_b_b_in': _L1_attn_b_in['b_in'], 'L1_attn_b_w_out': _L1_attn_b_in['w_out'], 'L1_attn_b_b_out': _L1_attn_b_in['b_out'], 'L1_ffn_gate_w': _L1_ffn_in['gate_w'], 'L1_ffn_gate_bias': _L1_ffn_in['gate_bias'], 'L1_ffn_Wu': _L1_ffn_in['Wu'], 'L1_ffn_bu': _L1_ffn_in['bu'], 'L1_ffn_Wd': _L1_ffn_in['Wd'], 'L1_ffn_bd': _L1_ffn_in['bd'], 'L1_ffn_sWu': _L1_ffn_in['sWu'], 'L1_ffn_sbu': _L1_ffn_in['sbu'], 'L1_ffn_sWd': _L1_ffn_in['sWd'], 'L1_ffn_sbd': _L1_ffn_in['sbd']}
    _x0 = _d['L0_attn_a_x']
    _d['L0_attn_a_x'] = jax.random.normal(jax.random.fold_in(jax.random.key(seed), 1), (1, 2048, 128), dtype=_x0.dtype)
    del _x0
    return _d

def reference(L0_attn_a_x, L0_attn_b_W_qkv, L0_attn_b_b_qkv, L0_attn_b_W_out, L0_attn_b_b_out, L0_ffn_Wr, L0_ffn_br, L0_ffn_W1, L0_ffn_b1, L0_ffn_W2, L0_ffn_b2, L0_ffn_W3, L0_ffn_b3, L1_attn_a_Wq, L1_attn_a_bq, L1_attn_a_Wk, L1_attn_a_bk, L1_attn_a_Wv, L1_attn_a_bv, L1_attn_a_Wo, L1_attn_a_bo, L1_attn_a_nrope_freq, L1_attn_b_w_in, L1_attn_b_b_in, L1_attn_b_w_out, L1_attn_b_b_out, L1_ffn_gate_w, L1_ffn_gate_bias, L1_ffn_Wu, L1_ffn_bu, L1_ffn_Wd, L1_ffn_bd, L1_ffn_sWu, L1_ffn_sbu, L1_ffn_sWd, L1_ffn_sbd):

    def _L0_attn_a_ref(x):
        import jax, jax.numpy as jnp
        import numpy as np
        B, T, C = x.shape
        tril = jnp.tril(jnp.ones((T, T), dtype=jnp.float32))
        attn = jnp.where(tril == 0, -jnp.inf, jnp.zeros((T, T), dtype=jnp.float32))
        attn = jax.nn.softmax(attn, axis=-1)
        return jnp.einsum('ts,bsc->btc', attn, x)

    def _L0_attn_b_ref(x, W_qkv, b_qkv, W_out, b_out):
        import jax, jax.numpy as jnp
        import numpy as np
        from math import sqrt
        EMBED = 128
        HEADS = 16
        B, N, E = x.shape
        H = HEADS
        d = E // H
        qkv = x @ W_qkv + b_qkv
        q, k, v = jnp.split(qkv, 3, axis=2)
        q = q.reshape(B, N, H, d)
        k = k.reshape(B, N, H, d)
        v = v.reshape(B, N, H, d)
        energy = jnp.einsum('bqhe,bkhe->bqhk', q, k)
        attn = jax.nn.softmax(energy, axis=-1) / sqrt(E)
        out = jnp.einsum('bihv,bvhd->bihd', attn, v)
        out = out.reshape(B, N, E)
        return out @ W_out + b_out

    def _L0_ffn_ref(x, Wr, br, W1, b1, W2, b2, W3, b3):
        import jax, jax.numpy as jnp
        import numpy as np
        E, D, DFF = (8, 128, 512)
        b, s, d = x.shape
        xt = x.reshape(b * s, d)
        logits = xt @ Wr + br
        pr, idx = jax.lax.top_k(logits, 2)
        w = jax.nn.softmax(pr, axis=-1)
        onehot = jax.nn.one_hot(idx, W1.shape[0], dtype=x.dtype)
        cw = jnp.einsum('tk,tke->te', w, onehot)
        y = jnp.zeros_like(xt)
        for e in range(W1.shape[0]):
            h = jax.nn.silu(xt @ W1[e] + b1[e]) * (xt @ W2[e] + b2[e])
            y = y + (h @ W3[e] + b3[e]) * cw[:, e:e + 1]
        return y.reshape(b, s, d)

    def _L1_attn_a_ref(x, Wq, bq, Wk, bk, Wv, bv, Wo, bo, nrope_freq):
        import jax, jax.numpy as jnp
        import numpy as np
        BASE_FREQUENCY = 10000.0
        LRP = 17
        MIN_L = 1.0 - LRP / 100.0
        SDT_L = (BASE_FREQUENCY - MIN_L * BASE_FREQUENCY) * 2.0
        ARM_ATTENTION = 2.0
        HEADS_DIM = 64

        def _nrope(xs, base, angle_range):
            N, T, d = xs.shape
            half = d // 2
            inv_freq = base ** (-jnp.arange(half, dtype=jnp.float32) / half)
            pos = jnp.arange(T, dtype=jnp.float32)
            scale = angle_range / jnp.maximum(T - 1, 1)
            ang = pos[:, None] * inv_freq[None, :] * scale
            cos, sin = (jnp.cos(ang), jnp.sin(ang))
            x1, x2 = (xs[..., :half], xs[..., half:])
            return jnp.concatenate([x1 * cos - x2 * sin, x1 * sin + x2 * cos], axis=-1)
        B, T, E = x.shape
        HD = HEADS_DIM
        H = E // HD
        half = HD // 2
        q = (x @ Wq + bq).reshape(B, T, H, HD).transpose(0, 2, 1, 3)
        k = (x @ Wk + bk).reshape(B, T, H, HD).transpose(0, 2, 1, 3)
        v = (x @ Wv + bv).reshape(B, T, H, HD).transpose(0, 2, 1, 3)
        q_content, q_spatial = (q[..., :half], q[..., half:])
        k_content, k_spatial = (k[..., :half], k[..., half:])
        base = jax.nn.sigmoid(nrope_freq[0]) * SDT_L + MIN_L * BASE_FREQUENCY
        rng = ARM_ATTENTION * jnp.pi
        q_spatial = _nrope(q_spatial.reshape(B * H, T, half), base, rng).reshape(B, H, T, half)
        k_spatial = _nrope(k_spatial.reshape(B * H, T, half), base, rng).reshape(B, H, T, half)
        q = jnp.concatenate([q_content, q_spatial], axis=-1)
        k = jnp.concatenate([k_content, k_spatial], axis=-1)
        score = jnp.einsum('bhqd,bhkd->bhqk', q, k) / jnp.sqrt(jnp.float32(HD))
        attn = jax.nn.softmax(score, axis=-1)
        out = jnp.einsum('bhqk,bhkd->bhqd', attn, v)
        out = out.transpose(0, 2, 1, 3).reshape(B, T, E)
        return out @ Wo + bo

    def _L1_attn_b_ref(x, w_in, b_in, w_out, b_out):
        import jax, jax.numpy as jnp
        import numpy as np
        N_HEAD = 16
        WINDOW = 128
        CAUSAL = False

        def _window_attention(x, w_in, b_in, w_out, b_out):
            B, T, D = x.shape
            H = N_HEAD
            hd = D // H
            scale = 1.0 / jnp.sqrt(jnp.float32(hd))
            qkv = jnp.einsum('btd,ed->bte', x, w_in) + b_in
            q, k, v = jnp.split(qkv, 3, axis=-1)
            q = q.reshape(B, T, H, hd).transpose(0, 2, 1, 3)
            k = k.reshape(B, T, H, hd).transpose(0, 2, 1, 3)
            v = v.reshape(B, T, H, hd).transpose(0, 2, 1, 3)
            scores = jnp.einsum('bhqd,bhkd->bhqk', q, k) * scale
            idx = jnp.arange(T)
            diff = idx[:, None] - idx[None, :]
            if CAUSAL:
                allowed = (diff >= 0) & (diff <= WINDOW)
            else:
                allowed = jnp.abs(diff) <= WINDOW
            NEG = jnp.float32(-1e+30)
            scores = jnp.where(allowed[None, None, :, :], scores, NEG)
            attn = jax.nn.softmax(scores, axis=-1)
            ctx = jnp.einsum('bhqk,bhkd->bhqd', attn, v)
            ctx = ctx.transpose(0, 2, 1, 3).reshape(B, T, D)
            out = jnp.einsum('btd,ed->bte', ctx, w_out) + b_out
            return x + out
        return _window_attention(x, w_in, b_in, w_out, b_out)

    def _L1_ffn_ref(x, gate_w, gate_bias, Wu, bu, Wd, bd, sWu, sbu, sWd, sbd):
        import jax, jax.numpy as jnp
        import numpy as np
        B, S, H, E, K = (2, 128, 128, 8, 2)
        F = 4 * H
        b, s, h = x.shape
        x_flat = x.reshape(-1, h)
        T = x_flat.shape[0]
        scores = jax.nn.sigmoid(x_flat @ gate_w.T + gate_bias)
        top_scores, top_idx = jax.lax.top_k(scores, K)
        top_scores = top_scores / (top_scores.sum(-1, keepdims=True) + 1e-06)
        w = jnp.zeros((T, E), x.dtype).at[jnp.arange(T)[:, None], top_idx].add(top_scores)
        h1 = jnp.einsum('th,efh->etf', x_flat, Wu) + bu[:, None, :]
        a1 = jax.nn.gelu(h1, approximate=False)
        y = jnp.einsum('etf,ehf->eth', a1, Wd) + bd[:, None, :]
        combined = jnp.einsum('te,eth->th', w, y)
        sh = jax.nn.gelu(x_flat @ sWu.T + sbu, approximate=False)
        shared = (sh @ sWd.T + sbd) * 0.1
        return (combined + shared).reshape(b, s, h)
    x = L0_attn_a_x
    x = x + _L0_attn_a_ref(_layernorm(x, axis=-1))
    x = x + _L0_ffn_ref(_layernorm(x, axis=-1), L0_ffn_Wr, L0_ffn_br, L0_ffn_W1, L0_ffn_b1, L0_ffn_W2, L0_ffn_b2, L0_ffn_W3, L0_ffn_b3)
    x = x + _L0_attn_b_ref(_layernorm(x, axis=-1), L0_attn_b_W_qkv, L0_attn_b_b_qkv, L0_attn_b_W_out, L0_attn_b_b_out)
    x = x + _L0_ffn_ref(_layernorm(x, axis=-1), L0_ffn_Wr, L0_ffn_br, L0_ffn_W1, L0_ffn_b1, L0_ffn_W2, L0_ffn_b2, L0_ffn_W3, L0_ffn_b3)
    x = x + _L1_attn_a_ref(_layernorm(x, axis=-1), L1_attn_a_Wq, L1_attn_a_bq, L1_attn_a_Wk, L1_attn_a_bk, L1_attn_a_Wv, L1_attn_a_bv, L1_attn_a_Wo, L1_attn_a_bo, L1_attn_a_nrope_freq)
    x = x + _L1_ffn_ref(_layernorm(x, axis=-1), L1_ffn_gate_w, L1_ffn_gate_bias, L1_ffn_Wu, L1_ffn_bu, L1_ffn_Wd, L1_ffn_bd, L1_ffn_sWu, L1_ffn_sbu, L1_ffn_sWd, L1_ffn_sbd)
    x = x + _L1_attn_b_ref(_layernorm(x, axis=-1), L1_attn_b_w_in, L1_attn_b_b_in, L1_attn_b_w_out, L1_attn_b_b_out)
    x = x + _L1_ffn_ref(_layernorm(x, axis=-1), L1_ffn_gate_w, L1_ffn_gate_bias, L1_ffn_Wu, L1_ffn_bu, L1_ffn_Wd, L1_ffn_bd, L1_ffn_sWu, L1_ffn_sbu, L1_ffn_sWd, L1_ffn_sbd)
    return x

_drawn_inputs = setup_inputs


def setup_inputs(seed=0):
    import zlib

    import numpy as np

    out = dict(_drawn_inputs(seed))
    spreads = {'L0_ffn_br': (0.0, 0.1),
     'L0_ffn_b1': (0.0, 0.736),
     'L0_ffn_b2': (0.0, 0.701),
     'L0_ffn_b3': (0.0, 0.1),
     'L1_attn_a_bq': (0.0, 0.8),
     'L1_attn_a_bk': (0.0, 0.8),
     'L1_attn_a_bv': (0.0, 0.33),
     'L1_attn_a_bo': (0.0, 0.1),
     'L1_ffn_gate_bias': (0.0, 0.1),
     'L1_ffn_bu': (0.0, 0.314),
     'L1_ffn_bd': (0.0, 0.1),
     'L1_ffn_sbu': (0.0, 0.8),
     'L1_ffn_sbd': (0.0, 0.544)}
    factors = {'L0_attn_b_b_qkv': 8.0,
     'L0_attn_b_b_out': 4.201,
     'L0_ffn_W1': 2.856,
     'L0_ffn_W2': 2.854,
     'L1_attn_a_Wq': 8.0,
     'L1_attn_a_Wk': 8.0,
     'L1_attn_a_Wv': 6.325,
     'L1_attn_b_w_in': 8.0,
     'L1_attn_b_b_in': 8.0,
     'L1_attn_b_w_out': 8.0,
     'L1_attn_b_b_out': 5.374,
     'L1_ffn_sWu': 6.998,
     'L1_ffn_sWd': 6.261}
    for name, (base, spread) in spreads.items():
        noise = np.random.default_rng([zlib.crc32(name.encode()), seed]).standard_normal(out[name].shape)
        drawn = base * np.exp(spread * noise) if base else spread * noise
        out[name] = jnp.asarray(drawn.astype(out[name].dtype))
    for name, factor in factors.items():
        out[name] = (out[name] * factor).astype(out[name].dtype)
    return out
```

```python
from contextlib import ExitStack

import numpy as np

import concourse.bass as bass
from concourse import mybir

F32 = mybir.dt.float32
F32R = mybir.dt.float32r
BF16 = mybir.dt.bfloat16
FP16 = mybir.dt.float16
I32 = mybir.dt.int32
U32 = mybir.dt.uint32
ALU = mybir.AluOpType
ACT = mybir.ActivationFunctionType
AX = mybir.AxisListType

P = 128
D = 128
T = 2048
NT = T // P
BANK = 512
LN_EPS = 1e-5

E = 8
K = 2
DFF = 512
FC = DFF // P
SLOT_TILES = (T * K + E * (P - 1)) // P
BIG = 3.0e38

HEADS = 16
HD = D // HEADS
ROWS = 3 * 3 * HD
AUG = ROWS + 3
WINDOW = 128
NEG = -1e30


class Named:
    pass


class Step:

    def __init__(self, n, c, ring, rounds=1):
        self.n, self.c, self.ring, self.rounds = n, c, ring, rounds
        self.j = n * (rounds * ring) + c
        self.s = c % ring
        self.turn = n * rounds + (c // ring + 1)

    def shifted(self, k):
        return Step(self.n, self.c + k, self.ring, self.rounds)

    def is_at(self, j):
        return isinstance(self.n, int) and self.j == j

    def below(self, j):
        return isinstance(self.n, int) and self.j < j


def chain(engine, sem, state):
    def link(instruction):
        state[0] += 1
        instruction.then_inc(sem, 1)
        engine.wait_ge(sem, state[0])
        return instruction
    return link


def start(nc, m, A, w):
    loaded = m.sem("inputs_loaded")
    made = m.sem("constants_made")
    with nc.Block() as block:

        @block.gpsimd
        def _(pool):
            link = chain(pool, made, [0])
            link(nc.gpsimd.memset(m.take[:, SLOT_TILES:], 0))
            link(nc.gpsimd.memset(m.ident[:], 0.0))
            link(nc.gpsimd.affine_select(out=m.ident[:], in_=m.ident[:], compare_op=ALU.not_equal, fill=1.0,
                                         base=0, pattern=[[-1, P]], channel_multiplier=1))
            link(nc.gpsimd.memset(m.ones[:], 1.0))
            link(nc.gpsimd.affine_select(out=m.upto[:], in_=m.ones[:], compare_op=ALU.is_ge, fill=0.0,
                                         base=0, pattern=[[1, P]], channel_multiplier=-1))
            link(nc.gpsimd.iota(m.token_id[:], pattern=[[P, NT]], base=0, channel_multiplier=1))
            link(nc.gpsimd.iota(m.index_i[:], pattern=[[1, P]], base=0, channel_multiplier=0))
            link(nc.gpsimd.iota(m.spare_i[:], pattern=[[P, SLOT_TILES]], base=(K + 1) * T, channel_multiplier=1))
            link(nc.gpsimd.memset(m.far_f[:], 0.0))
            link(nc.gpsimd.affine_select(out=m.far_f[:, 0:P], in_=m.far_f[:, 0:P], compare_op=ALU.is_ge, fill=NEG,
                                         base=0, pattern=[[1, P]], channel_multiplier=-1))
            link(nc.gpsimd.affine_select(out=m.far_f[:, 2 * P:], in_=m.far_f[:, 2 * P:], compare_op=ALU.is_ge, fill=NEG,
                                         base=0, pattern=[[-1, P]], channel_multiplier=1))
            link(nc.gpsimd.iota(m.tile_first_i[:], pattern=[[P, NT]], base=0, channel_multiplier=0))

        @block.sync
        def _(sp):
            sp.dma_start(m.x[:], A["L0_attn_a_x"].rearrange("b (i p) d -> p (b i) d", p=P)).then_inc(loaded, 16)
            for layer, (r, b) in enumerate((("L0_ffn_Wr", "L0_ffn_br"), ("L1_ffn_gate_wT", "L1_ffn_gate_bias"))):
                sp.dma_start(m.router[:, layer, :], A[r]).then_inc(loaded, 16)
                sp.dma_start(m.router_b[:, layer, :], A[b].partition_broadcast(P)).then_inc(loaded, 16)
            sp.wait_ge(loaded, 5 * 16)
            for dst, src in w.transfers:
                sp.dma_start(dst, src).then_inc(m.weights_loaded, 16)

        @block.vector
        def _(dve):
            dve.wait_ge(made, 12)
            link = chain(dve, m.dve_order, m.dve_count)
            link(nc.vector.tensor_copy(m.ident_bf[:], m.ident[:]))
            link(nc.vector.tensor_copy(m.ones_bf[:], m.ones[:]))
            link(nc.vector.tensor_tensor(m.before_bf[:], m.upto[:], m.ident[:], ALU.subtract))
            link(nc.vector.tensor_copy(m.index[:], m.index_i[:]))
            link(nc.vector.tensor_copy(m.token_f[:], m.token_id[:]))
            link(nc.vector.tensor_copy(m.far[:], m.far_f[:]))
            link(nc.vector.tensor_copy(m.spare_row[:], m.spare_i[:]))
            link(nc.vector.tensor_copy(m.tile_first[:], m.tile_first_i[:]))
            link(nc.vector.tensor_scalar(m.mean_w[:], m.token_f[:], 1.0, None, ALU.add))
            link(nc.vector.reciprocal(m.mean_w[:], m.mean_w[:]))
            link(nc.vector.tensor_scalar(m.expert_rank[:], m.index[:, 0:E], -1.0, float(E), ALU.mult, ALU.add))
            dve.wait_ge(loaded, 5 * 16)
            tile_statistics(nc, m, range(NT))


def tile_statistics(nc, m, tiles):
    for i in tiles:
        nc.vector.bn_stats(m.bn[:, i, :], m.x[:, i, :])


def layernorm(nc, m, name, store=False):
    std_ready = m.sem(f"{name}_std_ready")
    var_ready = m.sem(f"{name}_var_ready")
    rstd_ready = m.sem(f"{name}_rstd_ready")
    dve_tiles = m.sem(f"{name}_tiles_by_dve")
    act_tiles = m.sem(f"{name}_tiles_by_act")
    bank_ready = m.sem(f"{name}_bank_ready")
    bank_out = m.sem(f"{name}_bank_out")
    stored = m.sem(f"{name}_stored")
    mean, var, tmp, rstd, diff, shift = (m.ln_stat[:, k, :] for k in range(6))
    BY_DVE = 3
    with nc.Block() as block:

        @block.vector
        def _(dve):
            link = chain(dve, m.dve_order, m.dve_count)
            nc.vector.tensor_tensor(mean, m.bn[:, :, 1], m.bn[:, :, 4], ALU.add)
            nc.vector.tensor_tensor(tmp, m.bn[:, :, 2], m.bn[:, :, 5], ALU.add)
            link(nc.vector.tensor_tensor(diff, m.bn[:, :, 1], m.bn[:, :, 4], ALU.subtract))
            nc.vector.tensor_scalar(mean, mean, 0.5, None, ALU.mult)
            nc.vector.tensor_scalar(tmp, tmp, 1.0 / D, LN_EPS, ALU.mult, ALU.add)
            link(nc.vector.scalar_tensor_tensor(out=diff, in0=diff, scalar=0.25, in1=diff, op0=ALU.mult, op1=ALU.mult))
            nc.vector.tensor_tensor(var, diff, tmp, ALU.add).then_inc(var_ready, 1)
            dve.wait_ge(std_ready, 1)
            link(nc.vector.reciprocal(rstd, var))
            nc.vector.scalar_tensor_tensor(out=shift, in0=mean, scalar=-1.0, in1=rstd, op0=ALU.mult, op1=ALU.mult
                                           ).then_inc(rstd_ready, 1)
            for i in range(NT):
                if i % 4 < BY_DVE:
                    nc.vector.tensor_scalar(m.xn[:, i, :], m.x[:, i, :], mean[:, i:i + 1], rstd[:, i:i + 1],
                                            ALU.subtract, ALU.mult).then_inc(dve_tiles, 1)

        @block.scalar
        def _(act):
            nc.scalar.activation(m.idle[:], m.ones[:, 0:1], ACT.Sqrt)
            act.wait_ge(var_ready, 1)
            nc.scalar.activation(var, var, ACT.Sqrt).then_inc(std_ready, 1)
            act.wait_ge(rstd_ready, 1)
            for b in range(NT // 4):
                for i in range(4 * b + BY_DVE, 4 * b + 4):
                    nc.scalar.activation(m.xn[:, i, :], m.x[:, i, :], ACT.Identity, bias=shift[:, i:i + 1],
                                         scale=rstd[:, i:i + 1]).then_inc(act_tiles, 1)
            for b in range(NT // 4):
                act.wait_ge(bank_ready, b + 1)
                nc.scalar.copy(m.xnT[:, b * BANK:(b + 1) * BANK], m.ps[:, b, :]).then_inc(bank_out, 1)

        @block.tensor
        def _(pe):
            for i in range(NT):
                b = i // 4
                if i % 4 < BY_DVE:
                    pe.wait_ge(dve_tiles, b * BY_DVE + i % 4 + 1)
                else:
                    pe.wait_ge(act_tiles, b * (4 - BY_DVE) + i % 4 - BY_DVE + 1)
                last = nc.tensor.transpose(m.ps[:, i // 4, (i % 4) * P:(i % 4 + 1) * P], m.xn[:, i, :], m.ident[:])
                if i % 4 == 3:
                    last.then_inc(bank_ready, 1)

        if store:
            @block.sync
            def _(sp):
                for b in range(NT // 4):
                    sp.wait_ge(dve_tiles, (b + 1) * BY_DVE)
                    sp.wait_ge(act_tiles, (b + 1) * (4 - BY_DVE))
                    sp.dma_start(m.xn_dram.rearrange("(i p) d -> p i d", p=P)[:, 4 * b:4 * b + 4, :],
                                 m.xn[:, 4 * b:4 * b + 4, :]).then_inc(stored, 16)
    return stored, 16 * (NT // 4)


def causal_mean(nc, m, attention_transfers):
    sum_ready = m.sem("mean_prefix_ready")
    mean_ready = m.sem("mean_sum_ready")
    mean_used = m.sem("mean_sum_used")
    prefix = m.tok2
    with nc.Block() as block:

        @block.sync
        def _(sp):
            for dst, src in attention_transfers:
                sp.dma_start(dst, src).then_inc(m.attn_loaded, 16)

        @block.gpsimd
        def _(pool):
            nc.gpsimd.tensor_copy(prefix[:, 0, :], m.xn[:, 0, :]).then_inc(sum_ready, 1)
            for i in range(1, NT - 1):
                pool.wait_ge(sum_ready, i)
                nc.gpsimd.tensor_tensor(prefix[:, i, :], prefix[:, i - 1, :], m.xn[:, i, :], ALU.add).then_inc(sum_ready, 1)

        @block.tensor
        def _(pe):
            for i in range(NT):
                out = m.ps[:, i % 4, 0:P]
                if i >= 4:
                    pe.wait_ge(mean_used, i - 3)
                last = nc.tensor.matmul(out, m.upto[:], m.xn[:, i, :], start=True, stop=(i == 0))
                if i:
                    pe.wait_ge(sum_ready, i)
                    last = nc.tensor.matmul(out, m.ones[:], prefix[:, i - 1, :], start=False, stop=True)
                last.then_inc(mean_ready, 1)

        @block.vector
        def _(dve):
            for i in range(NT):
                dve.wait_ge(mean_ready, i + 1)
                nc.vector.scalar_tensor_tensor(out=m.x[:, i, :], in0=m.ps[:, i % 4, 0:P], scalar=m.mean_w[:, i:i + 1],
                                               in1=m.x[:, i, :], op0=ALU.mult, op1=ALU.add).then_inc(mean_used, 1)
                if i:
                    dve.wait_ge(mean_used, i)
                    tile_statistics(nc, m, [i - 1])
            dve.wait_ge(mean_used, NT)
            tile_statistics(nc, m, [NT - 1])


def route(nc, m, name, w, load, xn_stored, xn_count):
    logits_ready = m.sem(f"{name}_logits_ready")
    exp_asked = m.sem(f"{name}_exp_asked")
    exp_ready = m.sem(f"{name}_exp_ready")
    chosen_ready = m.sem(f"{name}_chosen_ready")
    rank_ready = m.sem(f"{name}_rank_ready")
    rows_ready = m.sem(f"{name}_row_onehots")
    hot_ready = m.sem(f"{name}_tile_onehots")
    tokens_ready = m.sem(f"{name}_tokens_ready")
    choices_ready = m.sem(f"{name}_choices_ready")
    onehot_used = m.sem(f"{name}_onehot_used")
    table_ready = m.sem(f"{name}_table_ready")
    up_ready = m.sem(f"{name}_shared_up_ready")
    act_ready = m.sem(f"{name}_shared_act_ready")
    down_ready = m.sem(f"{name}_shared_down_ready")
    down_used = m.sem(f"{name}_shared_down_used")
    NE = NT * E
    logits_ps = m.ps[:, 0, 0:NE]
    rank_ps = m.ps[:, 1, 0:NE + E]
    table_ps = m.ps[:, 2, 0:2 * SLOT_TILES]
    CH = 4
    KI = K * NT
    with ExitStack() as ctx, nc.Block() as block:
        def sb(n, shape, dt=F32):
            return ctx.enter_context(nc.sbuf_tensor(f"{name}_{n}", shape, dt))

        score = sb("score", [P, NT, E])
        cand = sb("cand", [P, NT, E])
        rest = sb("rest", [P, NT, E])
        chosen = sb("chosen", [P, K, NT, E])
        both = sb("both", [P, NT, E])
        cum = [sb("cum_a", [P, NT, E]), sb("cum_b", [P, NT, E])]
        both_bf = sb("both_bf", [P, NT, E], BF16)
        before = sb("before", [P, NT + 1, E], BF16)
        top = sb("top", [P, K, NT])
        small = sb("small", [P, 4, NT])
        place = sb("place", [P, NT, E])
        more = sb("more", [P, E, NT])
        start = [sb("start_a", [P, E]), sb("start_b", [P, E]), sb("start_c", [P, E])]
        slot = sb("slot", [P, K, NT])
        slot_i = sb("slot_i", [P, 3, KI], I32)
        slot_tile = sb("slot_tile", [P, KI])
        slot_row = sb("slot_row", [P, KI])
        row_hot = sb("row_hot", [P, 2, KI // CH, P], FP16)
        tile_hot = sb("tile_hot", [P, 2, KI // CH, 2, SLOT_TILES], FP16)
        hot = sb("hot", [P, 2, KI // CH, SLOT_TILES])
        passed = sb("passed", [P, SLOT_TILES, E])
        table = sb("table", [P, 3, SLOT_TILES])
        shared_a = sb("shared_a", [P, 2, FC, BANK]) if w.shared else None

        def block_steps(b):
            return [(b, f) for f in range(FC)] + [(b, "down")]

        between = [block_steps(2)[0:2], block_steps(2)[2:4], block_steps(2)[4:], block_steps(3)]

        @block.tensor
        def _(pe):
            for i in range(NT):
                last = nc.tensor.matmul(m.ps[:, 0, i * E:(i + 1) * E], m.xnT[:, i * P:(i + 1) * P], w.router,
                                        start=True, stop=True)
            last.then_inc(logits_ready, 1)

            def shared_expert(steps):
                for b, f in steps if w.shared else []:
                    if f != "down":
                        n = b * FC + f
                        if n == 0:
                            pe.wait_ge(m.shared_loaded, w.shared.loads)
                        if n >= 2:
                            pe.wait_ge(act_ready, n - 1)
                        nc.tensor.matmul(m.ps[:, 3 + n % 2, :], w.shared.up[:, f * P:(f + 1) * P],
                                         m.xnT[:, b * BANK:(b + 1) * BANK], start=True, stop=True).then_inc(up_ready, 1)
                        continue
                    if b >= 3:
                        pe.wait_ge(down_used, b - 2)
                    pe.wait_ge(act_ready, (b + 1) * FC)
                    for c in range(4):
                        for f in range(FC):
                            last = nc.tensor.matmul(m.ps[:, 5 + b % 3, c * D:(c + 1) * D],
                                                    shared_a[:, b % 2, f, c * P:(c + 1) * P],
                                                    w.shared.down[:, f, :], start=(f == 0), stop=(f == FC - 1))
                    last.then_inc(down_ready, 1)

            shared_expert(block_steps(0))
            pe.wait_ge(chosen_ready, 1)
            nc.tensor.matmul(rank_ps, m.ones_bf[:], before[:].rearrange("p i e -> p (i e)"), start=True, stop=False)
            nc.tensor.matmul(rank_ps[:, 0:NE], m.before_bf[:], both_bf[:].rearrange("p i e -> p (i e)"),
                             start=False, stop=True).then_inc(rank_ready, 1)
            shared_expert(block_steps(1))
            for c in range(CH):
                pe.wait_ge(rows_ready, c + 1)
                pe.wait_ge(tokens_ready, c + 1)
                pe.wait_ge(choices_ready, c + 1)
                for j in range(KI // CH):
                    last = nc.tensor.matmul(table_ps, row_hot[:, c % 2, j, :],
                                            tile_hot[:, c % 2, j, :, :].rearrange("p a s -> p (a s)"),
                                            start=(c == 0 and j == 0), stop=(c == CH - 1 and j == KI // CH - 1))
                last.then_inc(onehot_used, 1)
                shared_expert(between[c])

        @block.scalar
        def _(act):
            act.wait_ge(exp_asked, 1)
            if w.sigmoid:
                nc.scalar.activation(score[:], score[:], ACT.Exp, scale=-1.0).then_inc(exp_ready, 1)
            else:
                nc.scalar.activation(small[:, 1, :], small[:, 0, :], ACT.Exp).then_inc(exp_ready, 1)

            def activate(steps):
                for b, f in steps if w.shared else []:
                    if f == "down":
                        continue
                    n = b * FC + f
                    act.wait_ge(up_ready, n + 1)
                    if n == 0:
                        act.wait_ge(m.shared_loaded, w.shared.loads)
                    if b >= 2:
                        act.wait_ge(down_ready, b - 1)
                    nc.scalar.activation(shared_a[:, b % 2, f, :], m.ps[:, 3 + n % 2, :], ACT.Gelu,
                                         bias=w.shared.up_b[:, f:f + 1]).then_inc(act_ready, 1)

            activate(block_steps(0))
            activate(block_steps(1))
            for c in range(CH):
                act.wait_ge(hot_ready, c + 1)
                if c >= 2:
                    act.wait_ge(onehot_used, c - 1)
                nc.scalar.mul(tile_hot[:, c % 2, :, 1, :], hot[:, c % 2], float(c * KI // CH // NT + 1)
                              ).then_inc(choices_ready, 1)
                activate(between[c])

        @block.gpsimd
        def _(pool):
            for c in range(CH):
                first = c * KI // CH % NT
                pool.wait_ge(hot_ready, c + 1)
                if c >= 2:
                    pool.wait_ge(onehot_used, c - 1)
                nc.gpsimd.tensor_tensor(tile_hot[:, c % 2, :, 0, :], hot[:, c % 2],
                                        m.token_f[:, first:first + KI // CH].unsqueeze(2).to_broadcast([P, KI // CH, SLOT_TILES]),
                                        ALU.mult).then_inc(tokens_ready, 1)

        @block.sync
        def _(sp):
            for dst, src in w.transfers if load else []:
                sp.dma_start(dst, src).then_inc(m.weights_loaded, 16)
            sp.wait_ge(xn_stored, xn_count)

        @block.vector
        def _(dve):
            link = chain(dve, m.dve_order, m.dve_count)

            def over_tiles(a):
                return a.unsqueeze(1).to_broadcast([P, NT, E])

            def over_experts(a):
                return a.unsqueeze(2).to_broadcast([P, NT, E])

            dve.wait_ge(logits_ready, 1)
            add_bias = nc.vector.tensor_tensor(score[:], logits_ps.rearrange("p (i e) -> p i e", e=E),
                                               over_tiles(w.router_b), ALU.add)
            if w.sigmoid:
                add_bias.then_inc(exp_asked, 1)
                dve.wait_ge(exp_ready, 1)
                link(nc.vector.tensor_scalar(score[:], score[:], 1.0, None, ALU.add))
                link(nc.vector.reciprocal(score[:], score[:]))
            else:
                link(add_bias)

            def choose(k, scores):
                link(nc.vector.tensor_reduce(top[:, k, :], scores, AX.X, ALU.max))
                link(nc.vector.tensor_tensor(cand[:], scores, over_experts(top[:, k, :]), ALU.is_equal))
                link(nc.vector.tensor_tensor(cand[:], cand[:], over_tiles(m.expert_rank[:]), ALU.mult))
                link(nc.vector.tensor_reduce(small[:, 3, :], cand[:], AX.X, ALU.max))
                link(nc.vector.tensor_tensor(chosen[:, k, :, :], cand[:], over_experts(small[:, 3, :]), ALU.is_equal))

            choose(0, score[:])
            link(nc.vector.scalar_tensor_tensor(out=rest[:], in0=chosen[:, 0, :, :], scalar=-BIG, in1=score[:],
                                                op0=ALU.mult, op1=ALU.add))
            choose(1, rest[:])
            if not w.sigmoid:
                nc.vector.tensor_tensor(small[:, 0, :], top[:, 1, :], top[:, 0, :], ALU.subtract).then_inc(exp_asked, 1)

            link(nc.vector.tensor_tensor(both[:], chosen[:, 0, :, :], chosen[:, 1, :, :], ALU.add))
            nc.vector.tensor_copy(both_bf[:], both[:])
            prev = both
            for n, step in enumerate((1, 2, 4, 8)):
                nxt = cum[n % 2]
                nc.vector.tensor_copy(nxt[:, 0:step, :], prev[:, 0:step, :])
                link(nc.vector.tensor_tensor(nxt[:, step:NT, :], prev[:, step:NT, :], prev[:, 0:NT - step, :], ALU.add))
                prev = nxt
            nc.vector.tensor_copy(before[:, NT, :], prev[:, NT - 1, :])
            nc.vector.tensor_tensor(before[:, 0:NT, :], prev[:], both[:], ALU.subtract).then_inc(chosen_ready, 1)

            if w.sigmoid:
                link(nc.vector.tensor_tensor(small[:, 0, :], top[:, 0, :], top[:, 1, :], ALU.add))
                link(nc.vector.tensor_scalar(small[:, 0, :], small[:, 0, :], 1e-6, None, ALU.add))
                link(nc.vector.reciprocal(small[:, 1, :], small[:, 0, :]))
                for k in range(K):
                    nc.vector.tensor_tensor(m.gate[:, k, :], top[:, k, :], small[:, 1, :], ALU.mult)
            else:
                dve.wait_ge(exp_ready, 1)
                link(nc.vector.tensor_scalar(small[:, 2, :], small[:, 1, :], 1.0, None, ALU.add))
                link(nc.vector.reciprocal(m.gate[:, 0, :], small[:, 2, :]))
                nc.vector.tensor_tensor(m.gate[:, 1, :], m.gate[:, 0, :], small[:, 1, :], ALU.mult)

            dve.wait_ge(rank_ready, 1)
            link(nc.vector.tensor_tensor(more[:], rank_ps[:, NE:NE + E].unsqueeze(2).to_broadcast([P, E, NT]),
                                         m.tile_first[:].unsqueeze(1).to_broadcast([P, E, NT]), ALU.is_gt))
            link(nc.vector.tensor_reduce(start[0][:], more[:], AX.X, ALU.add))
            nc.vector.tensor_copy(start[2][:], start[0][:])
            a, b = start[0], start[1]
            for step in (1, 2, 4):
                nc.vector.tensor_copy(b[:, 0:step], a[:, 0:step])
                link(nc.vector.tensor_tensor(b[:, step:E], a[:, step:E], a[:, 0:E - step], ALU.add))
                a, b = b, a
            link(nc.vector.tensor_tensor(passed[:], a[:].unsqueeze(1).to_broadcast([P, SLOT_TILES, E]),
                                         m.index[:, 0:SLOT_TILES].unsqueeze(2).to_broadcast([P, SLOT_TILES, E]), ALU.is_le))
            link(nc.vector.tensor_reduce(table[:, 0, :], passed[:], AX.X, ALU.add))
            link(nc.vector.tensor_scalar(m.tile_expert[:], table[0:1, 0, :], float(E - 1), None, ALU.min))
            link(nc.vector.tensor_tensor(b[:], a[:], start[2][:], ALU.subtract))
            link(nc.vector.tensor_scalar(b[:], b[:], float(P), None, ALU.mult))
            link(nc.vector.tensor_tensor(place[:], rank_ps[:, 0:NE].rearrange("p (i e) -> p i e", e=E),
                                         over_tiles(b[:]), ALU.add))
            for k in range(K):
                link(nc.vector.tensor_tensor(cand[:], place[:], chosen[:, k, :, :], ALU.mult))
                link(nc.vector.tensor_reduce(slot[:, k, :], cand[:], AX.X, ALU.add))
            link(nc.vector.tensor_copy(slot_i[:, 0, :], slot[:].rearrange("p k i -> p (k i)")))
            nc.vector.tensor_scalar(slot_i[:, 1, :], slot_i[:, 0, :], 7, None, ALU.logical_shift_right)
            link(nc.vector.tensor_scalar(slot_i[:, 2, :], slot_i[:, 0, :], P - 1, None, ALU.bitwise_and))
            nc.vector.tensor_copy(slot_row[:], slot_i[:, 2, :])
            link(nc.vector.tensor_copy(slot_tile[:], slot_i[:, 1, :]))

            N = KI // CH
            for c in range(CH):
                lo, hi = c * N, (c + 1) * N
                if c >= 2:
                    dve.wait_ge(onehot_used, c - 1)
                    dve.wait_ge(tokens_ready, c - 1)
                    dve.wait_ge(choices_ready, c - 1)
                nc.vector.tensor_tensor(hot[:, c % 2], m.index[:, 0:SLOT_TILES].unsqueeze(1).to_broadcast([P, N, SLOT_TILES]),
                                        slot_tile[:, lo:hi].unsqueeze(2).to_broadcast([P, N, SLOT_TILES]), ALU.is_equal
                                        ).then_inc(hot_ready, 1)
                nc.vector.tensor_tensor(row_hot[:, c % 2, :, :], m.index[:].unsqueeze(1).to_broadcast([P, N, P]),
                                        slot_row[:, lo:hi].unsqueeze(2).to_broadcast([P, N, P]), ALU.is_equal
                                        ).then_inc(rows_ready, 1)
            dve.wait_ge(onehot_used, CH)
            link(nc.vector.tensor_copy(table[:, 0:2, :].rearrange("p a s -> p (a s)"), table_ps))
            nc.vector.tensor_copy(m.take[:, 0:SLOT_TILES], table[:, 0, :])
            link(nc.vector.tensor_scalar(table[:, 2, :], table[:, 1, :], 0.0, None, ALU.is_equal))
            link(nc.vector.tensor_tensor(table[:, 2, :], table[:, 2, :], m.spare_row[:], ALU.mult))
            link(nc.vector.scalar_tensor_tensor(out=table[:, 1, :], in0=table[:, 1, :], scalar=float(T),
                                                in1=table[:, 0, :], op0=ALU.mult, op1=ALU.add))
            link(nc.vector.scalar_tensor_tensor(out=table[:, 1, :], in0=table[:, 1, :], scalar=float(-T),
                                                in1=table[:, 2, :], op0=ALU.add, op1=ALU.add))
            link(nc.vector.tensor_copy(m.put[:], table[:, 1, :]))

            if w.shared:
                for b in range(NT // 4):
                    tiles = m.x[:, 4 * b:4 * b + 4, :]
                    out = m.tok2[:, 4 * b:4 * b + 4, :]
                    dve.wait_ge(down_ready, b + 1)
                    if b == 0:
                        dve.wait_ge(m.shared_loaded, w.shared.loads)
                    nc.vector.tensor_tensor(out, m.ps[:, 5 + b % 3, :].rearrange("p (c d) -> p c d", d=D),
                                            w.shared.down_b.unsqueeze(1).to_broadcast([P, 4, D]), ALU.add
                                            ).then_inc(down_used, 1)
                    dve.wait_ge(down_used, b + 1)
                    nc.vector.scalar_tensor_tensor(out=tiles, in0=out, scalar=0.1, in1=tiles,
                                                   op0=ALU.mult, op1=ALU.add)


def experts(nc, m, name, w):
    RING = 4
    gathered = [m.sem(f"{name}_gathered{r}") for r in range(RING)]
    scattered = [m.sem(f"{name}_scattered{r}") for r in range(RING)]
    take_ready = m.sem(f"{name}_take_ready")
    put_ready = m.sem(f"{name}_put_ready")
    xT_ready = m.sem(f"{name}_xT_ready")
    xT_copied = m.sem(f"{name}_xT_copied")
    h1_ready = m.sem(f"{name}_h1_ready")
    h2_ready = m.sem(f"{name}_h2_ready")
    h1_biased = m.sem(f"{name}_h1_biased")
    h2_biased = m.sem(f"{name}_h2_biased")
    act_ready = m.sem(f"{name}_act_ready")
    a_ready = m.sem(f"{name}_a_ready")
    aT_ready = m.sem(f"{name}_aT_ready")
    aT_copied = m.sem(f"{name}_aT_copied")
    y_ready = m.sem(f"{name}_y_ready")
    y_copied = m.sem(f"{name}_y_copied")
    first_added = m.sem(f"{name}_first_added")
    second_scaled = m.sem(f"{name}_second_scaled")
    second_added = m.sem(f"{name}_second_added")
    y_loaded = [m.sem(f"{name}_y_loaded{c}") for c in range(NT // 4)]
    gated = w.w2_of is not None
    act_done = act_ready if gated else a_ready
    LAST = SLOT_TILES - 1
    LAG = 1 if gated else 2
    FIRST = 2 * RING + LAG
    ROUNDS = 2
    AHEAD = RING - 1
    LOOPS = (SLOT_TILES - AHEAD - FIRST) // (ROUNDS * RING)
    with ExitStack() as ctx, nc.Block() as block:
        def sb(n, shape, dt=F32):
            return ctx.enter_context(nc.sbuf_tensor(f"{name}_{n}", shape, dt))

        xs = sb("xs", [P, RING, D])
        take1 = sb("take1", [P, 2, RING], I32)
        put1 = sb("put1", [P, 2, RING], I32)
        xsT = sb("xsT", [P, 2, P])
        h1 = sb("h1", [P, 2, DFF])
        h2 = sb("h2", [P, 2, DFF])
        act1 = sb("act1", [P, 2, DFF])
        aT = sb("aT", [P, 2, DFF])
        ys = sb("ys", [P, RING, D])
        y_in = [sb(f"y{k}", [P, NT, D]) for k in range(K)]
        xT_ps, aT_ps, y_ps = m.ps[:, 4, 0:P], m.ps[:, 5, :], m.ps[:, 6, 0:D]
        a = h2 if gated else act1

        def steps(engine, step):
            known = {}
            for j in range(FIRST):
                step(Step(0, j, RING), known)
            with engine.Fori(0, LOOPS) as n:
                known = {}
                for c in range(ROUNDS * RING):
                    step(Step(n, FIRST + c, RING, ROUNDS), known)
            known = {}
            for j in range(FIRST + LOOPS * ROUNDS * RING, SLOT_TILES):
                step(Step(0, j, RING), known)

        def expert_of(engine, t, known):
            if t.c not in known:
                known[t.c] = engine.value_load(m.tile_expert[0:1, bass.ds(t.j, 1)], min_val=0, max_val=E - 1)
            return known[t.c]

        @block.tensor
        def _(pe):
            pe.wait_ge(m.weights_loaded, w.loads)

            def transpose_x(t):
                pe.wait_ge(gathered[t.s], t.turn * 16)
                if not t.is_at(0):
                    pe.wait_ge(xT_copied, t.j)
                nc.tensor.transpose(xT_ps, xs[:, t.s, :], m.ident[:]).then_inc(xT_ready, 1)

            def finish_a(t):
                pe.wait_ge(a_ready, t.j + 1)
                if not t.is_at(0):
                    pe.wait_ge(aT_copied, t.j)
                for f in range(FC):
                    last = nc.tensor.transpose(aT_ps[:, f * P:(f + 1) * P], a[:, t.s % 2, f * P:(f + 1) * P], m.ident[:])
                last.then_inc(aT_ready, 1)

            def finish_y(t, known):
                e = expert_of(pe, t, known)
                pe.wait_ge(aT_copied, t.j + 1)
                if not t.is_at(0):
                    pe.wait_ge(y_copied, t.j)
                for f in range(FC):
                    last = nc.tensor.matmul(y_ps, aT[:, t.s % 2, f * P:(f + 1) * P], w.w3_of(f, e),
                                            start=(f == 0), stop=(f == FC - 1))
                last.then_inc(y_ready, 1)

            def step(t, known):
                e = expert_of(pe, t, known)
                pe.wait_ge(xT_copied, t.j + 1)
                if not t.below(2):
                    pe.wait_ge(h1_biased, t.j - 1)
                nc.tensor.matmul(m.ps[:, t.s % 2, :], xsT[:, t.s % 2, :], w.w1_of(e), start=True,
                                 stop=True).then_inc(h1_ready, 1)
                if not t.below(LAG):
                    expert_of(pe, t.shifted(-LAG), known)
                if not t.is_at(LAST):
                    expert_of(pe, t.shifted(1), known)
                if not gated and not t.is_at(LAST):
                    transpose_x(t.shifted(1))
                if not gated and not t.below(LAG):
                    finish_y(t.shifted(-LAG), known)
                if not t.is_at(0):
                    finish_a(t.shifted(-1))
                if gated and not t.is_at(LAST):
                    transpose_x(t.shifted(1))
                if gated:
                    if not t.below(2):
                        pe.wait_ge(h2_biased, t.j - 1)
                    nc.tensor.matmul(m.ps[:, 2 + t.s % 2, :], xsT[:, t.s % 2, :], w.w2_of(e), start=True,
                                     stop=True).then_inc(h2_ready, 1)
                if gated and not t.below(LAG):
                    finish_y(t.shifted(-LAG), known)

            transpose_x(Step(0, 0, RING))
            steps(pe, step)
            if not gated:
                finish_y(Step(0, LAST - 1, RING), {})
            finish_a(Step(0, LAST, RING))
            finish_y(Step(0, LAST, RING), {})

        @block.vector
        def _(dve):
            dve.wait_ge(m.weights_loaded, w.loads)

            def copy_xT(t):
                dve.wait_ge(xT_ready, t.j + 1)
                if not t.below(2):
                    dve.wait_ge(h2_ready if gated else h1_ready, t.j - 1)
                nc.vector.tensor_copy(xsT[:, t.s % 2, :], xT_ps).then_inc(xT_copied, 1)

            def add_h_bias(t, e, ps, ready, bias, out, biased, out_used):
                dve.wait_ge(ready, t.j + 1)
                if not t.below(2):
                    dve.wait_ge(out_used, t.j - 1)
                nc.vector.tensor_tensor(out[:, t.s % 2, :], ps, bias(e), ALU.add).then_inc(biased, 1)

            def copy_y(t, known):
                e = expert_of(dve, t, known)
                dve.wait_ge(y_ready, t.j + 1)
                if not t.below(RING):
                    dve.wait_ge(scattered[t.s], t.turn * 16 - 16)
                nc.vector.tensor_tensor(ys[:, t.s, :], y_ps, w.b3_of(e), ALU.add).then_inc(y_copied, 1)

            def step(t, known):
                e = expert_of(dve, t, known)
                add_h_bias(t, e, m.ps[:, t.s % 2, :], h1_ready, w.b1_of, h1, h1_biased, act_done)
                if not t.is_at(LAST):
                    copy_xT(t.shifted(1))
                if gated:
                    add_h_bias(t, e, m.ps[:, 2 + t.s % 2, :], h2_ready, w.b2_of, h2, h2_biased, aT_ready)
                if gated:
                    dve.wait_ge(act_ready, t.j + 1)
                    dve.wait_ge(h2_biased, t.j + 1)
                    nc.vector.tensor_tensor(h2[:, t.s % 2, :], act1[:, t.s % 2, :], h2[:, t.s % 2, :],
                                            ALU.mult).then_inc(a_ready, 1)
                if not t.below(LAG):
                    copy_y(t.shifted(-LAG), known)

            copy_xT(Step(0, 0, RING))
            steps(dve, step)
            for j in range(SLOT_TILES - LAG, SLOT_TILES):
                copy_y(Step(0, j, RING), {})

            for c in range(NT // 4):
                dve.wait_ge(y_loaded[c], K * 16)
                for i in range(4 * c, 4 * c + 4):
                    nc.vector.scalar_tensor_tensor(out=m.x[:, i, :], in0=y_in[0][:, i, :], scalar=m.gate[:, 0, i:i + 1],
                                                   in1=m.x[:, i, :], op0=ALU.mult, op1=ALU.add).then_inc(first_added, 1)
                if c:
                    dve.wait_ge(second_added, c)
                    tile_statistics(nc, m, range(4 * c - 4, 4 * c))
            dve.wait_ge(second_added, NT // 4)
            tile_statistics(nc, m, range(NT - 4, NT))

        @block.scalar
        def _(act):
            def copy_aT(t):
                act.wait_ge(aT_ready, t.j + 1)
                if not t.below(2):
                    act.wait_ge(y_ready, t.j - 1)
                nc.scalar.copy(aT[:, t.s % 2, :], aT_ps).then_inc(aT_copied, 1)

            def step(t, _):
                if not t.is_at(0):
                    copy_aT(t.shifted(-1))
                act.wait_ge(h1_biased, t.j + 1)
                if not t.below(2):
                    act.wait_ge(a_ready if gated else aT_ready, t.j - 1)
                nc.scalar.activation(act1[:, t.s % 2, :], h1[:, t.s % 2, :], w.function).then_inc(act_done, 1)

            steps(act, step)
            copy_aT(Step(0, LAST, RING))
            for c in range(NT // 4):
                act.wait_ge(y_loaded[c], K * 16)
                for i in range(4 * c, 4 * c + 4):
                    nc.scalar.mul(y_in[1][:, i, :], y_in[1][:, i, :], m.gate[:, 1, i:i + 1]).then_inc(second_scaled, 1)

        @block.gpsimd
        def _(pool):
            def offsets(t, buffer, table, ready):
                half = t.c // RING % 2
                if t.s == 0:
                    count = min(RING, SLOT_TILES - t.j) if isinstance(t.j, int) else RING
                    nc.gpsimd.tensor_copy(buffer[:, half, 0:count], table[:, bass.ds(t.j, count)]).then_inc(ready, 1)
                    pool.wait_ge(ready, t.turn)
                return bass.IndirectOffsetOnAxis(buffer[:, half, t.s:t.s + 1], 0)

            def gather(t):
                if not t.below(RING):
                    pool.wait_ge(xT_ready, t.j - (RING - 1))
                rows = offsets(t, take1, m.take, take_ready)
                nc.gpsimd.nop(nofuse=True)
                nc.gpsimd.indirect_dma_start(out=xs[:, t.s, :], out_offset=None, in_=m.xn_dram, in_offset=rows
                                             ).then_inc(gathered[t.s], 16)

            def scatter(t):
                if t.s == 0 and not t.below(2 * RING):
                    for r in range(RING):
                        pool.wait_ge(scattered[r], t.turn * 16 - 32)
                rows = offsets(t, put1, m.put, put_ready)
                pool.wait_ge(y_copied, t.j + 1)
                nc.gpsimd.nop(nofuse=True)
                nc.gpsimd.indirect_dma_start(out=m.y_dram, out_offset=rows, in_=ys[:, t.s, :], in_offset=None
                                             ).then_inc(scattered[t.s], 16)

            def step(t, _):
                if not (t.is_at(LAST) or t.is_at(LAST - 1) or t.is_at(LAST - 2)):
                    gather(t.shifted(AHEAD))
                if not t.below(LAG):
                    scatter(t.shifted(-LAG))

            for j in range(AHEAD):
                gather(Step(0, j, RING))
            steps(pool, step)
            for j in range(SLOT_TILES - LAG, SLOT_TILES):
                scatter(Step(0, j, RING))
            for c in range(NT // 4):
                tiles = slice(4 * c, 4 * c + 4)
                pool.wait_ge(first_added, 4 * c + 4)
                pool.wait_ge(second_scaled, 4 * c + 4)
                nc.gpsimd.tensor_tensor(m.x[:, tiles, :], m.x[:, tiles, :], y_in[1][:, tiles, :], ALU.add
                                        ).then_inc(second_added, 1)
            pool.wait_ge(second_added, NT // 4)

        @block.sync
        def _(sp):
            for r in range(RING):
                sp.wait_ge(scattered[r], 16 * len(range(r, SLOT_TILES, RING)))
            y_rows = m.y_dram[0:K * T, :].rearrange("(k i p) d -> k p i d", k=K, p=P)
            for c in range(NT // 4):
                for k in range(K):
                    sp.dma_start(y_in[k][:, 4 * c:4 * c + 4, :], y_rows[k, :, 4 * c:4 * c + 4, :]).then_inc(y_loaded[c], 16)


def project_heads(nc, m, name, w):
    proj_ready = m.sem(f"{name}_proj_ready")
    proj_copied = m.sem(f"{name}_proj_copied")
    first_ready = m.sem(f"{name}_first_part_ready")
    left_ready = m.sem(f"{name}_left_ready")
    second_ready = m.sem(f"{name}_second_part_ready")
    third_ready = m.sem(f"{name}_third_part_ready")
    v_ready = m.sem(f"{name}_v_ready")
    v_copied = m.sem(f"{name}_v_copied")
    parts_stored = m.sem(f"{name}_parts_stored")
    x_added = m.sem(f"{name}_x_added")
    NB = T // BANK
    with ExitStack() as ctx, nc.Block() as block:
        value = ctx.enter_context(nc.sbuf_tensor(f"{name}_value", [P, 2, BANK], F32))
        left = ctx.enter_context(nc.sbuf_tensor(f"{name}_left", [P, 2, BANK], F32))
        parts = ctx.enter_context(nc.sbuf_tensor(f"{name}_parts", [P, 2, 3, T], BF16))

        @block.tensor
        def _(pe):
            pe.wait_ge(m.attn_loaded, w.loads)
            for n in range(2 * NB):
                nc.tensor.matmul(m.ps[:, n % 4, :], w.qkv[:, n // NB * D:(n // NB + 1) * D],
                                 m.xnT[:, n % NB * BANK:(n % NB + 1) * BANK], start=True, stop=True
                                 ).then_inc(proj_ready, 1)
                if n + 1 >= 4:
                    pe.wait_ge(first_ready, n - 2)
                if n >= 4:
                    for c in range(4):
                        i = 4 * (n - 4) + c
                        last = nc.tensor.matmul(m.ps[:, n, c * D:(c + 1) * D], m.xnT[:, i * P:(i + 1) * P],
                                                w.qkv[:, 2 * D:3 * D], start=True, stop=True)
                    last.then_inc(v_ready, 1)

        @block.scalar
        def _(act):
            def second_part(n):
                act.wait_ge(left_ready, n + 1)
                nc.scalar.copy(parts[:, n // NB, 1, n % NB * BANK:(n % NB + 1) * BANK], left[:, n % 2, :]
                               ).then_inc(second_ready, 1)

            act.wait_ge(m.attn_loaded, w.loads)
            for n in range(2 * NB):
                X, bank, bias = n // NB, m.ps[:, n % 4, :], w.qkv_b[:, n // NB:n // NB + 1]
                act.wait_ge(proj_ready, n + 1)
                if n >= 2:
                    act.wait_ge(left_ready, n - 1)
                nc.scalar.activation(value[:, n % 2, :], bank, ACT.Identity, bias=bias).then_inc(proj_copied, 1)
                nc.scalar.activation(parts[:, X, 0, n % NB * BANK:(n % NB + 1) * BANK], bank, ACT.Identity, bias=bias
                                     ).then_inc(first_ready, 1)
                if n:
                    second_part(n - 1)
            second_part(2 * NB - 1)

        @block.vector
        def _(dve):
            def third_part(n):
                X, cols = n // NB, slice(n % NB * BANK, (n % NB + 1) * BANK)
                dve.wait_ge(second_ready, n + 1)
                nc.vector.tensor_tensor(parts[:, X, 2, cols], left[:, n % 2, :], parts[:, X, 1, cols], ALU.subtract
                                        ).then_inc(third_ready, 1)

            dve.wait_ge(m.attn_loaded, w.loads)
            for n in range(2 * NB):
                X, cols = n // NB, slice(n % NB * BANK, (n % NB + 1) * BANK)
                dve.wait_ge(proj_copied, n + 1)
                dve.wait_ge(first_ready, n + 1)
                if n >= 2:
                    dve.wait_ge(third_ready, n - 1)
                nc.vector.tensor_tensor(left[:, n % 2, :], value[:, n % 2, :], parts[:, X, 0, cols], ALU.subtract
                                        ).then_inc(left_ready, 1)
                if n:
                    third_part(n - 1)
                if n >= 4:
                    dve.wait_ge(x_added, 2 if w.add_xn else 1)
                    dve.wait_ge(v_ready, n - 3)
                    nc.vector.tensor_tensor(m.v[:, 4 * (n - 4):4 * (n - 3), :],
                                            m.ps[:, n, :].rearrange("p (c d) -> p c d", d=D),
                                            w.v_b.unsqueeze(1).to_broadcast([P, 4, D]), ALU.add).then_inc(v_copied, 1)
            third_part(2 * NB - 1)
            dve.wait_ge(v_copied, NT // 4)

        @block.gpsimd
        def _(pool):
            pool.wait_ge(m.attn_loaded, w.loads)
            nc.gpsimd.tensor_tensor(m.x[:], m.x[:], w.out_b.unsqueeze(1).to_broadcast([P, NT, D]), ALU.add
                                    ).then_inc(x_added, 1)
            if w.add_xn:
                pool.wait_ge(x_added, 1)
                nc.gpsimd.tensor_tensor(m.x[:], m.x[:], m.xn[:], ALU.add).then_inc(x_added, 1)

        @block.sync
        def _(sp):
            for X in range(2):
                sp.wait_ge(third_ready, NB * (X + 1))
                for j in range(3):
                    sp.dma_start(m.parts_dram[X, j], parts[:, X, j, :]).then_inc(parts_stored, 16)
            sp.wait_ge(parts_stored, 6 * 16)


class FullHead:

    MAX_UNITS = NT * (T // BANK)
    EXP_UNITS = NT * (T // BANK)
    PV_GROUPS = NT
    P_RING, P_COLS = 4, T
    MASKED = False
    LATE_AT, COPY_AT, TURN_AT, NEG_AT = 2, 3, 8, 58
    EARLY, MAX_OVER = 8, 53

    @staticmethod
    def max_unit(u):
        return u // 4, slice(u % 4 * BANK, (u % 4 + 1) * BANK), None

    @staticmethod
    def exp_unit(v):
        cols = slice(v % 4 * BANK, (v % 4 + 1) * BANK)
        return v // 4, cols, None, cols, v // 4 % 4

    @staticmethod
    def groups_after(v):
        return max((v - 2) // 4, 0)

    @staticmethod
    def exps_before(g):
        return 4 * g + 4

    @staticmethod
    def groups_before(v):
        return v // 4 - 3

    @staticmethod
    def group(g):
        return [(q, slice(0, BANK), g, g % 4, slice(q * BANK, (q + 1) * BANK), g == 0, g == NT - 1) for q in range(4)]

    @staticmethod
    def out_tiles(attn):
        return attn.rearrange("p (g c) d -> p c g d", c=4)


class WindowHead:

    MAX_UNITS = NT
    EXP_UNITS = NT
    PV_GROUPS = NT // 4
    P_RING, P_COLS = 8, 3 * P
    MASKED = True
    LATE_AT, COPY_AT, TURN_AT, NEG_AT = 1, 2, 5, 11
    EARLY, MAX_OVER = 6, 10

    @staticmethod
    def near(i):
        lo, hi = max(i - 1, 0), min(i + 2, NT)
        return slice(lo * P, hi * P), slice((lo - i + 1) * P, (hi - i + 1) * P)

    @staticmethod
    def max_unit(u):
        return (u, *WindowHead.near(u))

    @staticmethod
    def exp_unit(v):
        tokens, mask = WindowHead.near(v)
        return v, tokens, mask, mask, v % 8

    @staticmethod
    def groups_after(v):
        return max((v - 2) // 4, 0)

    @staticmethod
    def exps_before(g):
        return min(4 * g + 5, NT)

    @staticmethod
    def groups_before(v):
        return (v - 7) // 4 + 1 if v >= 7 else min((v + 9) // 4, NT // 4 - 1) + 1 - NT // 4

    @staticmethod
    def group(g):
        out = []
        for near in (0, -1, 1):
            for q in range(4):
                i = 4 * g + q
                j = i + near
                if 0 <= j < NT:
                    last = 1 if i + 1 < NT else -1
                    out.append((q, slice(g * P, (g + 1) * P), j, j % 8, slice((1 - near) * P, (2 - near) * P),
                                near == 0, near == last))
        return out

    @staticmethod
    def out_tiles(attn):
        return attn.rearrange("p (c g) d -> p c g d", g=4)


def attend(nc, m, name, w, head):
    RING = 3
    stacked = [m.sem(f"{name}_stacked{r}") for r in range(RING)]
    ones_set = m.sem(f"{name}_ones_set")
    v_set = m.sem(f"{name}_v_set")
    v_ready = m.sem(f"{name}_head_v_ready")
    max_ready = m.sem(f"{name}_max_ready")
    max_taken = m.sem(f"{name}_max_taken")
    neg_order = m.sem(f"{name}_neg_order")
    neg_ready = m.sem(f"{name}_neg_ready")
    turned_neg = m.sem(f"{name}_turned_neg")
    neg_copied = m.sem(f"{name}_neg_copied")
    neg_rows = m.sem(f"{name}_neg_rows")
    scores_ready = m.sem(f"{name}_scores_ready")
    exp_ready = m.sem(f"{name}_exp_ready")
    pv_done = m.sem(f"{name}_pv_done")
    out_copied = m.sem(f"{name}_out_copied")
    turned_out = m.sem(f"{name}_turned_out")
    recip_ready = m.sem(f"{name}_recip_ready")
    out_used = m.sem(f"{name}_out_used")
    U, V, G = head.MAX_UNITS, head.EXP_UNITS, head.PV_GROUPS
    LAST = HEADS - 1
    BANKS = 3
    TURN_BANK, OUT_BANK = 6, 7
    VC = 32
    NEG_OPS = 5 if U > NT else 4

    def exp_bank(t, v):
        return m.ps[:, (t.c * V + v) % BANKS, :]

    def max_bank(t, u):
        return m.ps[:, BANKS + (t.c * U + u) % BANKS, :]

    def max_after(v):
        return min(head.EARLY + (v + 1) * (U - head.EARLY) // head.MAX_OVER, U)

    def early_after(v):
        return max(v + 1 - (V - head.EARLY), 0)

    with ExitStack() as ctx, nc.Block() as block:
        def sb(n, shape, dt=F32):
            return ctx.enter_context(nc.sbuf_tensor(f"{name}_{n}", shape, dt))

        qs = [sb(f"qs{r}", [AUG, T], BF16) for r in range(RING)]
        ks = [sb(f"ks{r}", [AUG, T], BF16) for r in range(RING)]
        vh = sb("vh", [P, RING, NT, VC])
        p = sb("p", [P, head.P_RING, head.P_COLS])
        part_max = sb("part_max", [P, U])
        top = sb("top", [P, NT])
        left = sb("left", [P, NT])
        neg = sb("neg", [P, 3, NT], BF16)
        neg_row = sb("neg_row", [3 * NT, P], BF16)
        out = sb("out", [P, BANK])
        recip = sb("recip", [P, 4, 4])
        turn_ps = m.ps[:, TURN_BANK, :]
        neg_ps = m.ps[0:3 * NT, TURN_BANK, 0:P // 2].bitcast(BF16)

        def steps(engine, step):
            loops = (HEADS - RING - 2) // RING
            for h in range(RING):
                step(Step(0, h, RING))
            with engine.Fori(0, loops) as n:
                for c in range(RING):
                    step(Step(n, RING + c, RING))
            for h in range(RING + loops * RING, HEADS):
                step(Step(0, h, RING))

        @block.sync
        def _(sp):
            def stack(t):
                if not t.below(RING):
                    sp.wait_ge(scores_ready, (t.j - 2) * V)
                rows = m.parts_dram[:, :, bass.ds(t.j * HD, HD), :]
                for i in range(3):
                    block_rows = slice(i * 3 * HD, (i + 1) * 3 * HD)
                    sp.dma_start(qs[t.s][block_rows, :],
                                 rows[0, i].unsqueeze(0).to_broadcast([3, HD, T])).then_inc(stacked[t.s], 16)
                    sp.dma_start(ks[t.s][block_rows, :],
                                 rows[1]).then_inc(stacked[t.s], 16)

            def put_neg(t):
                sp.wait_ge(neg_copied, t.j + 1)
                sp.dma_start(qs[t.s][ROWS:AUG, :].rearrange("a (i p) -> a i p", p=P), neg_row[:]
                             ).then_inc(neg_rows, 16)

            def step(t):
                if not t.is_at(LAST):
                    stack(t.shifted(1))
                put_neg(t)

            stack(Step(0, 0, RING))
            for r in range(RING):
                sp.dma_start(ks[r][ROWS:AUG, :].rearrange("a (i p) -> a i p", p=P), m.ones_bf[0:3 * NT, :]
                             ).then_inc(ones_set, 16)
            steps(sp, step)

        @block.gpsimd
        def _(pool):
            nc.gpsimd.memset(vh[:], 0.0).then_inc(v_set, 1)
            pool.wait_ge(v_set, 1)
            nc.gpsimd.memset(vh[:, :, :, HD:HD + 1], 1.0).then_inc(v_set, 1)
            pool.wait_ge(v_set, 2)

            def copy_v(t):
                if not t.below(RING):
                    pool.wait_ge(pv_done, (t.j - 2) * G)
                nc.gpsimd.tensor_copy(vh[:, t.s, :, 0:HD], m.v[:, :, bass.ds(t.j * HD, HD)]).then_inc(v_ready, 1)

            def step(t):
                if not t.is_at(LAST):
                    copy_v(t.shifted(1))

            copy_v(Step(0, 0, RING))
            steps(pool, step)

        @block.tensor
        def _(pe):
            def mask_sides(bank, mask):
                if mask.stop - mask.start == 3 * P:
                    sides = bank.rearrange("p (i t) -> p i t", t=P)[:, 0:3:2, :]
                    far = m.far[:].rearrange("p (i t) -> p i t", t=P)[:, 0:3:2, :]
                elif mask.start == 0:
                    sides, far = bank[:, 0:P], m.far[:, 0:P]
                else:
                    sides, far = bank[:, P:2 * P], m.far[:, 2 * P:]
                return nc.tensor.matmul(sides, m.ident_bf[:], far, start=False, stop=True)

            def take_max(t, u):
                qt, keys, mask = head.max_unit(u)
                bank = max_bank(t, u)[:, 0:keys.stop - keys.start]
                if u == 0:
                    pe.wait_ge(stacked[t.s], t.turn * 6 * 16)
                if not (t.is_at(0) and u < BANKS):
                    pe.wait_ge(max_taken, t.j * U + (u + 1 - BANKS))
                last = nc.tensor.matmul(bank, qs[t.s][0:ROWS, qt * P:(qt + 1) * P], ks[t.s][0:ROWS, keys],
                                        start=True, stop=not head.MASKED)
                if head.MASKED:
                    last = mask_sides(bank, mask)
                last.then_inc(max_ready, 1)

            def scores(t, v):
                kt, queries, mask, _, _ = head.exp_unit(v)
                bank = exp_bank(t, v)[:, 0:queries.stop - queries.start]
                if v == 0:
                    pe.wait_ge(neg_rows, (t.j + 1) * 16)
                if not (t.is_at(0) and v < BANKS):
                    pe.wait_ge(exp_ready, t.j * V + (v + 1 - BANKS))
                last = nc.tensor.matmul(bank, ks[t.s][:, kt * P:(kt + 1) * P], qs[t.s][:, queries],
                                        start=True, stop=not head.MASKED)
                if head.MASKED:
                    last = mask_sides(bank, mask)
                last.then_inc(scores_ready, 1)

            def weigh(t, g):
                if g == 0:
                    pe.wait_ge(v_ready, t.j + 1)
                    if not t.is_at(0):
                        pe.wait_ge(out_copied, t.j)
                pe.wait_ge(exp_ready, t.j * V + head.exps_before(g))
                for q, cols, kt, ring, p_cols, start, stop in head.group(g):
                    last = nc.tensor.matmul(m.ps[q * VC:(q + 1) * VC, OUT_BANK, cols], vh[:, t.s, kt, :],
                                            p[:, ring, p_cols], start=start, stop=stop)
                last.then_inc(pv_done, 1)

            def turn_neg(t):
                pe.wait_ge(neg_ready, t.j + 1)
                if not t.is_at(0):
                    pe.wait_ge(neg_copied, t.j)
                    pe.wait_ge(out_used, t.j - 1)
                nc.tensor.nop(nofuse=True)
                nc.tensor.transpose(neg_ps, neg[:].rearrange("p a i -> p (a i)"), m.ident_bf[:]).then_inc(turned_neg, 1)

            def turn_out(t):
                pe.wait_ge(out_copied, t.j + 1)
                pe.wait_ge(neg_copied, t.j + (1 if t.is_at(LAST) else 2))
                pe.wait_ge(out_used, t.j)
                for c in range(4):
                    last = nc.tensor.transpose(turn_ps[:, c * P:(c + 1) * P], out[:, c * P:(c + 1) * P], m.ident[:])
                last.then_inc(turned_out, 1)

            def step(t):
                more, behind = not t.is_at(LAST), not t.is_at(0)
                taken, early, groups = head.EARLY, 0, 0
                for v in range(V):
                    scores(t, v)
                    if behind and v == head.LATE_AT:
                        weigh(t.shifted(-1), G - 1)
                    if behind and v == head.TURN_AT:
                        turn_out(t.shifted(-1))
                    while more and taken < max_after(v):
                        take_max(t.shifted(1), taken)
                        taken += 1
                    if more and v == head.NEG_AT:
                        turn_neg(t.shifted(1))
                    while more and not t.is_at(LAST - 1) and early < early_after(v):
                        take_max(t.shifted(2), early)
                        early += 1
                    while groups < head.groups_after(v):
                        weigh(t, groups)
                        groups += 1

            pe.wait_ge(ones_set, RING * 16)
            for u in range(U):
                take_max(Step(0, 0, RING), u)
            turn_neg(Step(0, 0, RING))
            for u in range(head.EARLY):
                take_max(Step(0, 1, RING), u)
            steps(pe, step)
            weigh(Step(0, LAST, RING), G - 1)
            turn_out(Step(0, LAST, RING))

        @block.scalar
        def _(act):
            def copy_out(t):
                act.wait_ge(pv_done, (t.j + 1) * G)
                if not t.is_at(0):
                    act.wait_ge(turned_out, t.j)
                nc.scalar.copy(out[:], m.ps[:, OUT_BANK, :]).then_inc(out_copied, 1)

            def step(t):
                for v in range(V):
                    _, queries, _, p_cols, ring = head.exp_unit(v)
                    act.wait_ge(scores_ready, t.j * V + (v + 1))
                    if not (t.is_at(0) and head.groups_before(v) <= 0):
                        act.wait_ge(pv_done, t.j * G + head.groups_before(v))
                    nc.scalar.activation(p[:, ring, p_cols], exp_bank(t, v)[:, 0:queries.stop - queries.start], ACT.Exp,
                                         scale=w.scale).then_inc(exp_ready, 1)
                    if v == head.COPY_AT and not t.is_at(0):
                        copy_out(t.shifted(-1))

            steps(act, step)
            copy_out(Step(0, LAST, RING))

        @block.vector
        def _(dve):
            def reduce_max(t, u):
                _, keys, _ = head.max_unit(u)
                dve.wait_ge(max_ready, t.j * U + (u + 1))
                to = part_max if U > NT else top
                nc.vector.tensor_reduce(to[:, u:u + 1], max_bank(t, u)[:, 0:keys.stop - keys.start],
                                        AX.X, ALU.max).then_inc(max_taken, 1)

            def negate(t):
                done = [0]

                def link(instruction):
                    done[0] += 1
                    instruction.then_inc(neg_order, 1)
                    dve.wait_ge(neg_order, t.j * (NEG_OPS - 1) + done[0])

                dve.wait_ge(max_taken, (t.j + 1) * U)
                if not t.is_at(0):
                    dve.wait_ge(turned_neg, t.j)
                if U > NT:
                    link(nc.vector.tensor_reduce(top[:], part_max[:].rearrange("p (i b) -> p i b", i=NT), AX.X, ALU.max))
                link(nc.vector.tensor_scalar(neg[:, 0, :], top[:], -1.0, None, ALU.mult))
                link(nc.vector.scalar_tensor_tensor(out=left[:], in0=top[:], scalar=-1.0, in1=neg[:, 0, :],
                                                    op0=ALU.mult, op1=ALU.subtract))
                link(nc.vector.tensor_copy(neg[:, 1, :], left[:]))
                nc.vector.tensor_tensor(neg[:, 2, :], left[:], neg[:, 1, :], ALU.subtract).then_inc(neg_ready, 1)

            def copy_neg(t):
                dve.wait_ge(turned_neg, t.j + 1)
                if not t.is_at(0):
                    dve.wait_ge(neg_rows, t.j * 16)
                nc.vector.tensor_copy(neg_row[:], neg_ps).then_inc(neg_copied, 1)

            def normalize(t):
                sums = turn_ps.rearrange("p (c g r) -> p c g r", c=4, g=4)
                dve.wait_ge(turned_out, t.j + 1)
                nc.vector.reciprocal(recip[:], sums[:, :, :, HD]).then_inc(recip_ready, 1)
                dve.wait_ge(recip_ready, t.j + 1)
                nc.vector.tensor_tensor(head.out_tiles(m.attn[:, :, bass.ds(t.j * HD, HD)]), sums[:, :, :, 0:HD],
                                        recip[:].unsqueeze(3).to_broadcast([P, 4, 4, HD]), ALU.mult
                                        ).then_inc(out_used, 1)

            def step(t):
                if t.is_at(LAST):
                    normalize(t.shifted(-1))
                    return
                for u in range(head.EARLY, U):
                    if u == max_after(head.TURN_AT - 1) and not t.is_at(0):
                        normalize(t.shifted(-1))
                    reduce_max(t.shifted(1), u)
                negate(t.shifted(1))
                copy_neg(t.shifted(1))
                if not t.is_at(LAST - 1):
                    for u in range(head.EARLY):
                        reduce_max(t.shifted(2), u)

            for u in range(U):
                reduce_max(Step(0, 0, RING), u)
            negate(Step(0, 0, RING))
            copy_neg(Step(0, 0, RING))
            for u in range(head.EARLY):
                reduce_max(Step(0, 1, RING), u)
            steps(dve, step)
            normalize(Step(0, LAST, RING))


def project_out(nc, m, name, w):
    bank_ready = m.sem(f"{name}_turned")
    bank_copied = m.sem(f"{name}_turned_copied")
    y_ready = m.sem(f"{name}_y_ready")
    y_added = m.sem(f"{name}_y_added")
    with nc.Block() as block:

        @block.tensor
        def _(pe):
            for b in range(NT // 4 + 1):
                if b < NT // 4:
                    for c in range(4):
                        last = nc.tensor.transpose(m.ps[:, b, c * P:(c + 1) * P], m.attn[:, 4 * b + c, :], m.ident[:])
                    last.then_inc(bank_ready, 1)
                if b:
                    pe.wait_ge(bank_copied, b)
                    for c in range(4):
                        i = 4 * (b - 1) + c
                        last = nc.tensor.matmul(m.ps[:, 3 + b, c * D:(c + 1) * D], m.xnT[:, i * P:(i + 1) * P], w.out,
                                                start=True, stop=True)
                    last.then_inc(y_ready, 1)

        @block.scalar
        def _(act):
            for b in range(NT // 4):
                act.wait_ge(bank_ready, b + 1)
                nc.scalar.mul(m.xnT[:, b * BANK:(b + 1) * BANK], m.ps[:, b, :], w.out_scale).then_inc(bank_copied, 1)

        @block.vector
        def _(dve):
            for b in range(NT // 4):
                dve.wait_ge(y_ready, b + 1)
                tiles = m.x[:, 4 * b:4 * b + 4, :]
                nc.vector.tensor_tensor(tiles, m.ps[:, 4 + b, :].rearrange("p (c d) -> p c d", d=D), tiles,
                                        ALU.add).then_inc(y_added, 1)
                dve.wait_ge(y_added, b + 1)
                tile_statistics(nc, m, range(4 * b, 4 * b + 4))


WIDE_HEADS = 2
WHD = D // WIDE_HEADS
ROT = WHD // 4
BASE_FREQUENCY = 10000.0
MIN_L = 1.0 - 17 / 100.0
SDT_L = (BASE_FREQUENCY - MIN_L * BASE_FREQUENCY) * 2.0
ANGLE_RANGE = 2.0 * np.pi
PI_BELOW = 3.1415925


def rotary_tables(nc, m):
    asked = m.sem("rotary_asked")
    given = m.sem("rotary_given")
    with ExitStack() as ctx, nc.Block() as block:
        def sb(n, shape, dt=F32):
            return ctx.enter_context(nc.sbuf_tensor(f"rotary_{n}", shape, dt))

        one = sb("one", [P, 4])
        freq = sb("freq", [P, ROT])
        angle = sb("angle", [P, NT, ROT])
        half = sb("half", [P, NT, ROT])

        @block.vector
        def _(dve):
            link = chain(dve, m.dve_order, m.dve_count)
            dve.wait_ge(given, 1)
            link(nc.vector.tensor_scalar(one[:, 1:2], one[:, 0:1], 1.0, None, ALU.add))
            link(nc.vector.reciprocal(one[:, 1:2], one[:, 1:2]))
            nc.vector.tensor_scalar(one[:, 2:3], one[:, 1:2], SDT_L, MIN_L * BASE_FREQUENCY, ALU.mult, ALU.add
                                    ).then_inc(asked, 1)
            dve.wait_ge(given, 2)
            nc.vector.tensor_scalar(one[:, 3:4], one[:, 3:4], -1.0 / ROT, None, ALU.mult).then_inc(asked, 1)
            dve.wait_ge(given, 3)
            link(nc.vector.tensor_tensor(angle[:], m.token_f[:].unsqueeze(2).to_broadcast([P, NT, ROT]),
                                         freq[:].unsqueeze(1).to_broadcast([P, NT, ROT]), ALU.mult))
            link(nc.vector.tensor_scalar(angle[:], angle[:], ANGLE_RANGE / (T - 1), None, ALU.mult))
            link(nc.vector.tensor_scalar(half[:], angle[:], 0.5, PI_BELOW, ALU.mult, ALU.min))
            link(nc.vector.tensor_scalar(angle[:], angle[:], float(np.pi), PI_BELOW, ALU.subtract, ALU.min))
            nc.vector.tensor_scalar(angle[:], angle[:], -PI_BELOW, None, ALU.max).then_inc(asked, 1)
            dve.wait_ge(given, 5)
            nc.vector.tensor_scalar(m.sin[:], angle[:], -1.0, None, ALU.mult)
            link(nc.vector.tensor_tensor(half[:], half[:], half[:], ALU.mult))
            link(nc.vector.tensor_scalar(m.cos[:], half[:], -2.0, 1.0, ALU.mult, ALU.add))

        @block.scalar
        def _(act):
            act.wait_ge(m.attn_loaded, m.attn_loads)
            nc.scalar.activation(one[:, 0:1], m.nrope[:], ACT.Exp, scale=-1.0).then_inc(given, 1)
            act.wait_ge(asked, 1)
            nc.scalar.activation(one[:, 3:4], one[:, 2:3], ACT.Ln).then_inc(given, 1)
            act.wait_ge(asked, 2)
            nc.scalar.activation(freq[:], m.index[:, 0:ROT], ACT.Exp, scale=one[:, 3:4]).then_inc(given, 1)
            act.wait_ge(asked, 3)
            nc.scalar.activation(half[:], half[:], ACT.Sin).then_inc(given, 1)
            nc.scalar.activation(angle[:], angle[:], ACT.Sin).then_inc(given, 1)


HIGH_BITS = 0xFFFFF000


def project_wide(nc, m, name, w, c):
    proj_ready = m.sem(f"{name}_proj_ready")
    biased = m.sem(f"{name}_biased")
    products_ready = m.sem(f"{name}_products_ready")
    rotated = m.sem(f"{name}_rotated")
    split = [m.sem(f"{name}_split{r}") for r in range(2)]
    turned = m.sem(f"{name}_turned")
    turned_act = m.sem(f"{name}_turned_copied_by_act")
    turned_dve = m.sem(f"{name}_turned_copied_by_dve")
    x_added = m.sem(f"{name}_x_added")
    NB = NT // 4
    with ExitStack() as ctx, nc.Block() as block:
        qk = [ctx.enter_context(nc.sbuf_tensor(f"{name}_{x}", [P, NT, WIDE_HEADS, WHD], F32)) for x in "qk"]
        q_parts = ctx.enter_context(nc.sbuf_tensor(f"{name}_q_parts", [P, NT, WIDE_HEADS, 2, WHD], F32))
        k_parts = ctx.enter_context(nc.sbuf_tensor(f"{name}_k_parts", [P, NT, WIDE_HEADS, 2, 2, WHD], F32))
        tmp = [ctx.enter_context(nc.sbuf_tensor(f"{name}_tmp{x}", [P, 4, NT, WIDE_HEADS, ROT], F32)) for x in "qk"]
        banks = []
        for h in range(WIDE_HEADS):
            for b in range(NB):
                banks.append((0, h, b, None, c.q))
        for h in range(WIDE_HEADS):
            for b in range(NB):
                banks.append((1, h, b, 0, c.k_high))
                banks.append((1, h, b, 1, c.k_low))

        by_dve = [n % 3 == 2 for n in range(len(banks))]
        copied = [(turned_dve, sum(by_dve[:n + 1])) if by_dve[n] else (turned_act, n + 1 - sum(by_dve[:n + 1]))
                  for n in range(len(banks))]

        @block.tensor
        def _(pe):
            pe.wait_ge(m.attn_loaded, m.attn_loads)
            for n in range(3 * NB):
                if n >= 8:
                    pe.wait_ge(biased, n - 7)
                for c4 in range(4):
                    i = 4 * (n % NB) + c4
                    last = nc.tensor.matmul(m.ps[:, n % 8, c4 * D:(c4 + 1) * D], m.xnT[:, i * P:(i + 1) * P],
                                            w.qkv[:, n // NB * D:(n // NB + 1) * D], start=True, stop=True)
                last.then_inc(proj_ready, 1)
            pe.wait_ge(biased, 3 * NB)
            for n, (X, h, b, part, _) in enumerate(banks):
                pe.wait_ge(split[X], 2 * (h + 1))
                if n >= 8:
                    pe.wait_ge(*copied[n - 8])
                for c4 in range(4):
                    tile = q_parts[:, 4 * b + c4, h] if X == 0 else k_parts[:, 4 * b + c4, h, part]
                    last = nc.tensor.transpose(m.ps[:, n % 8, c4 * P:(c4 + 1) * P], tile.rearrange("p a d -> p (a d)"),
                                               m.ident[:])
                last.then_inc(turned, 1)

        @block.scalar
        def _(act):
            for n, (X, h, b, part, dst) in enumerate(banks):
                if not by_dve[n]:
                    act.wait_ge(turned, n + 1)
                    nc.scalar.copy(dst[:, h, b * BANK:(b + 1) * BANK], m.ps[:, n % 8, :]).then_inc(turned_act, 1)

        @block.vector
        def _(dve):
            link = chain(dve, m.dve_order, m.dve_count)
            dve.wait_ge(m.attn_loaded, m.attn_loads)
            for n in range(3 * NB):
                dve.wait_ge(proj_ready, n + 1)
                X, i = n // NB, 4 * (n % NB)
                dst = qk[X][:, i:i + 4].rearrange("p i h d -> p i (h d)") if X < 2 else c.v[:, i:i + 4, :]
                nc.vector.tensor_tensor(dst, m.ps[:, n % 8, :].rearrange("p (i d) -> p i d", d=D),
                                        w.b3[:, X, :].unsqueeze(1).to_broadcast([P, 4, D]), ALU.add).then_inc(biased, 1)
            nc.vector.tensor_tensor(c.twice[:], m.ident[:, 0:WHD], m.ident[:, WHD:P], ALU.add)

            dve.wait_ge(biased, NB)
            a, b = qk[0][:, :, :, 2 * ROT:3 * ROT], qk[0][:, :, :, 3 * ROT:4 * ROT]
            cos = m.cos[:].unsqueeze(2).to_broadcast([P, NT, WIDE_HEADS, ROT])
            sin = m.sin[:].unsqueeze(2).to_broadcast([P, NT, WIDE_HEADS, ROT])
            t = tmp[0]
            nc.vector.tensor_tensor(t[:, 0], a, cos, ALU.mult)
            nc.vector.tensor_tensor(t[:, 1], b, sin, ALU.mult)
            nc.vector.tensor_tensor(t[:, 2], a, sin, ALU.mult)
            link(nc.vector.tensor_tensor(t[:, 3], b, cos, ALU.mult))
            nc.vector.tensor_tensor(a, t[:, 0], t[:, 1], ALU.subtract)
            link(nc.vector.tensor_tensor(b, t[:, 2], t[:, 3], ALU.add))
            for X in range(2):
                if X:
                    dve.wait_ge(rotated, 2)
                for h in range(WIDE_HEADS):
                    if X == 0:
                        full, high, low = qk[0][:, :, h], q_parts[:, :, h, 0], q_parts[:, :, h, 1]
                    else:
                        full = qk[1][:, :, h].unsqueeze(2).to_broadcast([P, NT, 2, WHD])
                        high, low = k_parts[:, :, h, 0], k_parts[:, :, h, 1]
                    nc.vector.tensor_scalar(high.bitcast(U32), full.bitcast(U32), HIGH_BITS, None,
                                            ALU.bitwise_and).then_inc(split[X], 1)
                    dve.wait_ge(split[X], 2 * h + 1)
                    nc.vector.tensor_tensor(low, full, high, ALU.subtract).then_inc(split[X], 1)
            for n, (X, h, b, part, dst) in enumerate(banks):
                if by_dve[n]:
                    dve.wait_ge(turned, n + 1)
                    nc.vector.tensor_copy(dst[:, h, b * BANK:(b + 1) * BANK], m.ps[:, n % 8, :]).then_inc(turned_dve, 1)

        @block.gpsimd
        def _(pool):
            pool.wait_ge(m.attn_loaded, m.attn_loads)
            nc.gpsimd.tensor_tensor(m.x[:], m.x[:], w.out_b.unsqueeze(1).to_broadcast([P, NT, D]), ALU.add
                                    ).then_inc(x_added, 1)
            pool.wait_ge(biased, 2 * NB)
            a, b = qk[1][:, :, :, 2 * ROT:3 * ROT], qk[1][:, :, :, 3 * ROT:4 * ROT]
            cos = m.cos[:].unsqueeze(2).to_broadcast([P, NT, WIDE_HEADS, ROT])
            sin = m.sin[:].unsqueeze(2).to_broadcast([P, NT, WIDE_HEADS, ROT])
            t = tmp[1]
            nc.gpsimd.tensor_tensor(t[:, 0], a, cos, ALU.mult)
            nc.gpsimd.tensor_tensor(t[:, 1], b, sin, ALU.mult)
            nc.gpsimd.tensor_tensor(t[:, 2], a, sin, ALU.mult)
            nc.gpsimd.tensor_tensor(t[:, 3], b, cos, ALU.mult).then_inc(products_ready, 1)
            pool.wait_ge(products_ready, 1)
            nc.gpsimd.tensor_tensor(a, t[:, 0], t[:, 1], ALU.subtract).then_inc(rotated, 1)
            nc.gpsimd.tensor_tensor(b, t[:, 2], t[:, 3], ALU.add).then_inc(rotated, 1)
            pool.wait_ge(x_added, 1)


def attend_wide(nc, m, name, w, c):
    max_ready = m.sem(f"{name}_max_ready")
    max_taken = m.sem(f"{name}_max_taken")
    neg_ready = m.sem(f"{name}_neg_ready")
    turned_neg = m.sem(f"{name}_turned_neg")
    neg_copied = m.sem(f"{name}_neg_copied")
    zeroed = m.sem(f"{name}_zeroed")
    scores_ready = m.sem(f"{name}_scores_ready")
    exp_ready = m.sem(f"{name}_exp_ready")
    summed = m.sem(f"{name}_summed")
    pv_done = m.sem(f"{name}_pv_done")
    out_copied = m.sem(f"{name}_out_copied")
    turned_out = m.sem(f"{name}_turned_out")
    out_used = m.sem(f"{name}_out_used")
    QB = T // BANK
    ITEMS = WIDE_HEADS * QB
    U = 4 * QB
    PAIRS = NT // 2
    ADDS = NT - 1
    BANKS = 3
    TURN_BANK, OUT_BANK = 6, 7
    P_RING = 8
    COPY_AT, TURN_AT, NEG_AT, MAX_OVER = 1, 4, 13, 12
    with ExitStack() as ctx, nc.Block() as block:
        def sb(n, shape, dt=F32):
            return ctx.enter_context(nc.sbuf_tensor(f"{name}_{n}", shape, dt))

        p = sb("p", [P, P_RING, BANK])
        total = sb("total", [P, 2, BANK])
        part_max = sb("part_max", [P, U])
        top = sb("top", [P, 4])
        left = sb("left", [P, 4])
        neg = sb("neg", [P, 3, 4], BF16)
        neg_in = sb("neg_in", [P, 2, BANK], BF16)
        three = sb("three", [P, P], BF16)
        out = sb("out", [P, BANK])
        recip = sb("recip", [P, 2, 4])
        neg_ps = m.ps[0:3, TURN_BANK, :]
        out_ps = m.ps[:, TURN_BANK, 0:4 * WHD].rearrange("p (i d) -> p i d", d=WHD)
        sum_ps = m.ps[:, TURN_BANK, 4 * WHD:4 * WHD + 4]

        @block.gpsimd
        def _(pool):
            nc.gpsimd.memset(neg_in[:], 0.0).then_inc(zeroed, 1)
            nc.gpsimd.memset(three[:], 0.0).then_inc(zeroed, 1)
            pool.wait_ge(zeroed, 2)
            nc.gpsimd.memset(three[0:3, :], 1.0).then_inc(zeroed, 1)
            for n in range(ITEMS):
                sums = total[:, n % 2, :]
                if n >= 2:
                    pool.wait_ge(turned_out, n - 1)
                for kt in range(1, NT):
                    g = n * NT + kt
                    pool.wait_ge(exp_ready, g + 1)
                    if kt > 1:
                        pool.wait_ge(summed, n * ADDS + kt - 1)
                    before = p[:, (g - 1) % P_RING, :] if kt == 1 else sums
                    nc.gpsimd.tensor_tensor(sums, before, p[:, g % P_RING, :], ALU.add).then_inc(summed, 1)

        @block.tensor
        def _(pe):
            def take_max(n, u):
                h, qt, kb = n // QB, 4 * (n % QB) + u // QB, u % QB
                g = n * U + u
                if g >= BANKS:
                    pe.wait_ge(max_taken, g + 1 - BANKS)
                bank, q, keys = m.ps[:, BANKS + g % BANKS, :], c.q[:, h, qt * P:(qt + 1) * P], slice(kb * BANK, (kb + 1) * BANK)
                nc.tensor.matmul(bank, q, c.k_high[:, h, keys], start=True, stop=False)
                nc.tensor.matmul(bank, q, c.k_low[:, h, keys], start=False, stop=True).then_inc(max_ready, 1)

            def scores(n, kt):
                h, qb = n // QB, n % QB
                g = n * NT + kt
                bank, queries, keys = m.ps[:, g % BANKS, :], c.q[:, h, qb * BANK:(qb + 1) * BANK], slice(kt * P, (kt + 1) * P)
                if g >= BANKS:
                    pe.wait_ge(exp_ready, g + 1 - BANKS)
                if kt == 0:
                    pe.wait_ge(neg_copied, n + 1)
                nc.tensor.matmul(bank, c.k_high[:, h, keys], queries, start=True, stop=False)
                nc.tensor.matmul(bank, c.k_low[:, h, keys], queries, start=False, stop=False)
                nc.tensor.matmul(bank, three[:], neg_in[:, n % 2, :], start=False, stop=True).then_inc(scores_ready, 1)

            def weigh(pair):
                n, first = pair // PAIRS, pair % PAIRS * 2
                pe.wait_ge(exp_ready, 2 * pair + 2)
                if first == 0 and n:
                    pe.wait_ge(out_copied, n)
                for side in range(2):
                    last = nc.tensor.matmul(m.ps[side * WHD:(side + 1) * WHD, OUT_BANK, :],
                                            c.v[:, first + side, n // QB * WHD:(n // QB + 1) * WHD],
                                            p[:, (2 * pair + side) % P_RING, :], start=(first == 0), stop=(first == NT - 2))
                last.then_inc(pv_done, 1)

            def turn_neg(n):
                pe.wait_ge(neg_ready, n + 1)
                if n:
                    pe.wait_ge(neg_copied, n)
                if n >= 2:
                    pe.wait_ge(out_used, n - 1)
                for c4 in range(4):
                    last = nc.tensor.matmul(neg_ps[:, c4 * P:(c4 + 1) * P], neg[:, :, c4], m.ident_bf[:],
                                            start=True, stop=True)
                last.then_inc(turned_neg, 1)

            def turn_out(n):
                pe.wait_ge(out_copied, n + 1)
                pe.wait_ge(summed, (n + 1) * ADDS)
                pe.wait_ge(neg_copied, min(n + 2, ITEMS))
                if n:
                    pe.wait_ge(out_used, n)
                for c4 in range(4):
                    nc.tensor.matmul(out_ps[:, c4, :], out[:, c4 * P:(c4 + 1) * P], c.twice[:], start=True, stop=True)
                    last = nc.tensor.matmul(sum_ps[:, c4:c4 + 1], total[:, n % 2, c4 * P:(c4 + 1) * P], m.ones[:, 0:1],
                                            start=True, stop=True)
                last.then_inc(turned_out, 1)

            pe.wait_ge(zeroed, 3)
            for u in range(U):
                take_max(0, u)
            turn_neg(0)
            for n in range(ITEMS):
                more = n + 1 < ITEMS
                taken = 0
                for kt in range(NT):
                    g = n * NT + kt
                    scores(n, kt)
                    while more and taken < min((kt + 1) * U // MAX_OVER, U):
                        take_max(n + 1, taken)
                        taken += 1
                    if n and kt == TURN_AT:
                        turn_out(n - 1)
                    if g % 2 and g >= 3:
                        weigh((g - 3) // 2)
                    if more and kt == NEG_AT:
                        turn_neg(n + 1)
            weigh(ITEMS * PAIRS - 1)
            turn_out(ITEMS - 1)

        @block.scalar
        def _(act):
            def copy_out(n):
                act.wait_ge(pv_done, PAIRS * (n + 1))
                if n:
                    act.wait_ge(turned_out, n)
                nc.scalar.copy(out[:], m.ps[:, OUT_BANK, :]).then_inc(out_copied, 1)

            for n in range(ITEMS):
                for kt in range(NT):
                    g = n * NT + kt
                    act.wait_ge(scores_ready, g + 1)
                    if g >= P_RING:
                        old = g - P_RING
                        act.wait_ge(pv_done, old // 2 + 1)
                        act.wait_ge(summed, old // NT * ADDS + max(old % NT, 1))
                    nc.scalar.activation(p[:, g % P_RING, :], m.ps[:, g % BANKS, :], ACT.Exp, scale=w.scale).then_inc(exp_ready, 1)
                    if kt == COPY_AT and n:
                        copy_out(n - 1)
            copy_out(ITEMS - 1)

        @block.vector
        def _(dve):
            link = chain(dve, m.dve_order, m.dve_count)

            def reduce_max(n, u):
                g = n * U + u
                dve.wait_ge(max_ready, g + 1)
                nc.vector.tensor_reduce(part_max[:, u:u + 1], m.ps[:, BANKS + g % BANKS, :], AX.X, ALU.max
                                        ).then_inc(max_taken, 1)

            def negate(n):
                dve.wait_ge(max_taken, (n + 1) * U)
                if n:
                    dve.wait_ge(turned_neg, n)
                link(nc.vector.tensor_reduce(top[:], part_max[:].rearrange("p (i b) -> p i b", b=QB), AX.X, ALU.max))
                link(nc.vector.tensor_scalar(neg[:, 0, :], top[:], -1.0, None, ALU.mult))
                link(nc.vector.scalar_tensor_tensor(out=left[:], in0=top[:], scalar=-1.0, in1=neg[:, 0, :],
                                                    op0=ALU.mult, op1=ALU.subtract))
                link(nc.vector.tensor_copy(neg[:, 1, :], left[:]))
                nc.vector.tensor_tensor(neg[:, 2, :], left[:], neg[:, 1, :], ALU.subtract).then_inc(neg_ready, 1)
                dve.wait_ge(turned_neg, n + 1)
                if n == 0:
                    dve.wait_ge(zeroed, 1)
                if n >= 2:
                    dve.wait_ge(scores_ready, NT * (n - 1))
                nc.vector.tensor_copy(neg_in[0:3, n % 2, :], neg_ps).then_inc(neg_copied, 1)

            def normalize(n):
                h, qb = n // QB, n % QB
                dve.wait_ge(turned_out, n + 1)
                link(nc.vector.reciprocal(recip[:, n % 2, :], sum_ps))
                nc.vector.tensor_tensor(m.attn[:, 4 * qb:4 * qb + 4, h * WHD:(h + 1) * WHD], out_ps,
                                        recip[:, n % 2, :].unsqueeze(2).to_broadcast([P, 4, WHD]), ALU.mult
                                        ).then_inc(out_used, 1)

            for n in range(ITEMS):
                for u in range(U):
                    if n >= 2 and u == (TURN_AT + 1) * U // MAX_OVER:
                        normalize(n - 2)
                    reduce_max(n, u)
                negate(n)
            normalize(ITEMS - 2)
            normalize(ITEMS - 1)
            dve.wait_ge(out_used, ITEMS)


def attention_wide(nc, m, name, w):
    rotary_tables(nc, m)
    layernorm(nc, m, f"{name}_ln")
    with ExitStack() as ctx:
        c = Named()
        c.q = ctx.enter_context(nc.sbuf_tensor(f"{name}_q", [2 * WHD, WIDE_HEADS, T], F32R))
        c.k_high = ctx.enter_context(nc.sbuf_tensor(f"{name}_k_high", [2 * WHD, WIDE_HEADS, T], F32R))
        c.k_low = ctx.enter_context(nc.sbuf_tensor(f"{name}_k_low", [2 * WHD, WIDE_HEADS, T], F32R))
        c.v = ctx.enter_context(nc.sbuf_tensor(f"{name}_v", [P, NT, D], F32))
        c.twice = ctx.enter_context(nc.sbuf_tensor(f"{name}_twice", [P, WHD], F32))
        project_wide(nc, m, f"{name}_in", w, c)
        attend_wide(nc, m, name, w, c)
    project_out(nc, m, f"{name}_out", w)


def start_loads(nc, transfers, loaded):
    with nc.Block() as block:

        @block.sync
        def _(sp):
            for dst, src in transfers:
                sp.dma_start(dst, src).then_inc(loaded, 16)


def expert_weights(nc, m, A, layer, ctx, loads_before):
    def sb(name, shape):
        return ctx.enter_context(nc.sbuf_tensor(f"L{layer}_{name}", shape, F32))

    m.w1, m.b1 = sb("w1", [P, E, DFF]), sb("b1", [P, E, DFF])
    m.w3, m.b3 = sb("w3", [P, FC, E, D]), sb("b3", [P, E, D])
    m.w2 = sb("w2", [P, E if layer == 0 else 2, DFF])
    m.b2 = sb("b2", [P, E if layer == 0 else 2, DFF])
    w1 = m.w1[:].rearrange("p e f -> p (e f)")
    w2 = m.w2[:].rearrange("p e f -> p (e f)")
    w3 = m.w3[:].rearrange("p c e d -> p c (e d)")
    b1 = m.b1[:].rearrange("p e f -> p (e f)")
    b2 = m.b2[:].rearrange("p e f -> p (e f)")
    b3 = m.b3[:].rearrange("p e d -> p (e d)")

    def everywhere(a):
        flat = a.rearrange("e f -> (e f)") if len(a.shape) == 2 else a
        return flat.partition_broadcast(P)

    w = Named()
    w.w1_of = lambda e: w1[:, bass.ds(e * DFF, DFF)]
    w.w2_of = (lambda e: w2[:, bass.ds(e * DFF, DFF)]) if layer == 0 else None
    w.w3_of = lambda f, e: w3[:, f, bass.ds(e * D, D)]
    w.b1_of = lambda e: b1[:, bass.ds(e * DFF, DFF)]
    w.b2_of = lambda e: b2[:, bass.ds(e * DFF, DFF)]
    w.b3_of = lambda e: b3[:, bass.ds(e * D, D)]
    w.router, w.router_b, w.shared = m.router[:, layer, :], m.router_b[:, layer, :], None
    w.sigmoid, w.function = layer == 1, ACT.Silu if layer == 0 else ACT.Gelu
    if layer == 0:
        w.transfers = [(m.w1[:], A["L0_ffn_W1"].rearrange("e d f -> d e f")),
                       (m.w2[:], A["L0_ffn_W2"].rearrange("e d f -> d e f"))]
        w.transfers += [(m.w3[:, c], A["L0_ffn_W3"].rearrange("e (c p) d -> c p e d", p=P)[c]) for c in range(FC)]
        w.transfers += [(b1, everywhere(A["L0_ffn_b1"])), (b2, everywhere(A["L0_ffn_b2"])),
                        (b3, everywhere(A["L0_ffn_b3"]))]
    else:
        w.shared = Named()
        w.shared.up, w.shared.down = m.w2[:, 0, :], m.w2[:, 1, :].rearrange("p (c d) -> p c d", c=FC)
        w.shared.up_b, w.shared.down_b = m.b2[:, 0, 0:FC], m.b2[:, 1, 0:D]
        w.shared.transfers = [(w.shared.up, A["L1_ffn_sWuT"]),
                              (w.shared.down, A["L1_ffn_sWdT"].rearrange("(c p) d -> p c d", p=P)),
                              (w.shared.up_b, A["L1_ffn_sbuT"]), (w.shared.down_b, everywhere(A["L1_ffn_sbd"]))]
        w.shared.loads = 16 * len(w.shared.transfers)
        w.transfers = [(m.w1[:], A["L1_ffn_WuT"].rearrange("d (e f) -> d e f", e=E))]
        w.transfers += [(m.w3[:, c], A["L1_ffn_WdT"].rearrange("e (c p) d -> c p e d", p=P)[c]) for c in range(FC)]
        w.transfers += [(b1, everywhere(A["L1_ffn_bu"])), (b3, everywhere(A["L1_ffn_bd"]))]
    w.loads = loads_before + 16 * len(w.transfers)
    return w


def attention_weights(nc, m, A):
    ws = []
    todo = []
    for n, (qkv, qkv_b, out, out_b, scale, out_scale) in enumerate((
            ("L0_attn_b_W_qkv", "L0_attn_b_b_qkv", "L0_attn_b_W_out", "L0_attn_b_b_out", 1.0, D ** -0.5),
            ("L1_attn_b_w_inT", "L1_attn_b_b_in", "L1_attn_b_w_outT", "L1_attn_b_b_out", HD ** -0.5, 1.0))):
        w = Named()
        w.qkv, w.out = m.aw[:, n, 0:3 * D], m.aw[:, n, 3 * D:]
        w.qkv_b, w.v_b, w.out_b = m.aqb[:, n, :], m.avb[:, n, :], m.aob[:, n, :]
        w.scale, w.out_scale, w.add_xn = scale, out_scale, n == 1
        todo += [(w.qkv, A[qkv]), (w.out, A[out]), (w.qkv_b, A[qkv_b + "_qk"]),
                 (w.v_b, A[qkv_b][2 * D:].partition_broadcast(P)), (w.out_b, A[out_b].partition_broadcast(P))]
        ws.append(w)
    w = Named()
    w.qkv, w.out, w.b3, w.out_b = m.aw[:, 2, 0:3 * D], m.aw[:, 2, 3 * D:], m.ab3, m.aob[:, 2, :]
    w.scale, w.out_scale = WHD ** -0.5, 1.0
    for X, x in enumerate("qkv"):
        todo += [(w.qkv[:, X * D:(X + 1) * D], A[f"L1_attn_a_W{x}"]),
                 (w.b3[:, X, :], A[f"L1_attn_a_b{x}"].partition_broadcast(P))]
    todo += [(w.out, A["L1_attn_a_Wo"]), (w.out_b, A["L1_attn_a_bo"].partition_broadcast(P)),
             (m.nrope[:], A["L1_attn_a_nrope_freq"].partition_broadcast(P))]
    ws.append(w)
    m.attn_loads = 16 * len(todo)
    for w in ws:
        w.loads = m.attn_loads
    return ws, todo


def store(nc, m, out):
    stored = m.sem("output_stored")
    with nc.Block() as block:

        @block.sync
        def _(sp):
            sp.dma_start(out.rearrange("b (i p) d -> p (b i) d", p=P), m.x[:]).then_inc(stored, 16)
            sp.wait_ge(stored, 16)


def memory(nc, ctx):
    def sb(name, shape, dt=F32):
        return ctx.enter_context(nc.sbuf_tensor(name, shape, dt))

    m = Named()
    m.sem = nc.alloc_semaphore
    m.dve_order, m.dve_count = ctx.enter_context(nc.semaphore("dve_order")), [0]
    m.weights_loaded = ctx.enter_context(nc.semaphore("weights_loaded"))
    m.shared_loaded = ctx.enter_context(nc.semaphore("shared_loaded"))
    m.ps = ctx.enter_context(nc.psum_tensor("ps", [P, 8, BANK], F32))
    m.x = sb("x_res", [P, NT, D])
    m.xn = sb("xn", [P, NT, D])
    m.xnT = sb("xnT", [D, T])
    m.tok2 = sb("tok2", [P, NT, D])
    m.bn = sb("bn", [P, NT, 6])
    m.ln_stat = sb("ln_stat", [P, 6, NT])
    m.idle = sb("idle", [P, 1])
    m.ident = sb("ident", [P, P])
    m.ident_bf = sb("ident_bf", [P, P], BF16)
    m.ones = sb("ones", [P, P])
    m.ones_bf = sb("ones_bf", [P, P], BF16)
    m.upto = sb("upto", [P, P])
    m.before_bf = sb("before_bf", [P, P], BF16)
    m.token_id = sb("token_id", [P, NT], I32)
    m.token_f = sb("token_f", [P, NT])
    m.mean_w = sb("mean_w", [P, NT])
    m.index_i = sb("index_i", [P, P], I32)
    m.index = sb("index", [P, P])
    m.tile_first = sb("tile_first", [P, NT])
    m.tile_first_i = sb("tile_first_i", [P, NT], I32)
    m.spare_i = sb("spare_i", [P, SLOT_TILES], I32)
    m.spare_row = sb("spare_row", [P, SLOT_TILES])
    m.expert_rank = sb("expert_rank", [P, E])
    m.gate = sb("gate", [P, K, NT])
    m.take = sb("take", [P, SLOT_TILES + 3], I32)
    m.put = sb("put", [P, SLOT_TILES], I32)
    m.tile_expert = sb("tile_expert", [1, SLOT_TILES], I32)
    m.router = sb("router", [P, 2, E])
    m.router_b = sb("router_b", [P, 2, E])
    m.far_f = sb("far_f", [P, 3 * P])
    m.far = sb("far", [P, 3 * P], BF16)
    m.v = m.xn
    m.attn = m.tok2
    m.attn_loaded = ctx.enter_context(nc.semaphore("attn_loaded"))
    m.aw = sb("aw", [P, 3, 4 * D])
    m.aqb = sb("aqb", [P, 3, 2])
    m.avb = sb("avb", [P, 3, D])
    m.aob = sb("aob", [P, 3, D])
    m.ab3 = sb("ab3", [P, 3, D])
    m.nrope = sb("nrope", [P, 1])
    m.cos = sb("cos", [P, NT, ROT])
    m.sin = sb("sin", [P, NT, ROT])
    m.parts_dram = nc.dram_tensor("parts_scratch", (2, 3, D, T), BF16, kind="Internal").ap()
    m.xn_dram = nc.dram_tensor("xn_scratch", (T, D), F32, kind="Internal").ap()
    m.y_dram = nc.dram_tensor("y_scratch", (K * T + SLOT_TILES * P, D), F32, kind="Internal").ap()
    return m


def network(nc, A, out):
    with ExitStack() as ctx:
        m = memory(nc, ctx)
        (narrow0, narrow1, wide), attention_transfers = attention_weights(nc, m, A)
        with ExitStack() as layer0:
            w = expert_weights(nc, m, A, 0, layer0, 0)
            with nc.cleanup_on_exit():
                start(nc, m, A, w)
                layernorm(nc, m, "mean_ln")
                causal_mean(nc, m, attention_transfers)
            with nc.cleanup_on_exit():
                moe(nc, m, "moe0a", w)
            with nc.cleanup_on_exit():
                attention_narrow(nc, m, "full", narrow0, FullHead)
            with nc.cleanup_on_exit():
                moe(nc, m, "moe0b", w)
            loads = w.loads
        with nc.cleanup_on_exit():
            attention_wide(nc, m, "wide", wide)
        with ExitStack() as layer1:
            w = expert_weights(nc, m, A, 1, layer1, loads)
            start_loads(nc, w.shared.transfers, m.shared_loaded)
            with nc.cleanup_on_exit():
                moe(nc, m, "moe1a", w, load=True)
            with nc.cleanup_on_exit():
                attention_narrow(nc, m, "window", narrow1, WindowHead)
            with nc.cleanup_on_exit():
                moe(nc, m, "moe1b", w)
        with nc.cleanup_on_exit():
            store(nc, m, out)


def moe(nc, m, name, w, load=False):
    stored, count = layernorm(nc, m, f"{name}_ln", store=True)
    route(nc, m, f"{name}_route", w, load, stored, count)
    experts(nc, m, f"{name}_experts", w)


def attention_narrow(nc, m, name, w, head):
    layernorm(nc, m, f"{name}_ln")
    project_heads(nc, m, f"{name}_in", w)
    attend(nc, m, name, w, head)
    project_out(nc, m, f"{name}_out", w)


def kernel(**inputs):
    import numpy as _np
    import concourse.bacc as _bacc
    from concourse import mybir as _mybir
    from concourse.bass_utils import run_bass_kernel_spmd as _run

    a = {k: _np.asarray(v) for k, v in inputs.items()}
    for name in ("L1_ffn_gate_w", "L1_ffn_sWu", "L1_ffn_sWd", "L1_attn_b_w_in", "L1_attn_b_w_out"):
        a[name + "T"] = a.pop(name).T
    a["L1_ffn_WuT"] = a.pop("L1_ffn_Wu").transpose(2, 0, 1).reshape(D, E * DFF)
    a["L1_ffn_WdT"] = a.pop("L1_ffn_Wd").transpose(0, 2, 1)
    a["L1_ffn_sbuT"] = a.pop("L1_ffn_sbu").reshape(FC, P).T
    for name in ("L0_attn_b_b_qkv", "L1_attn_b_b_in"):
        a[name + "_qk"] = a[name][0:2 * D].reshape(2, D).T

    nc = _bacc.Bacc("TRN2", target_bir_lowering=False, num_devices=1)
    nc.disable_value_cache = True
    arrays, args = {}, {}
    for name, array in a.items():
        array = _np.ascontiguousarray(array)
        arrays[f"in_{name}"] = array
        args[name] = nc.dram_tensor(f"in_{name}", array.shape, _mybir.dt.from_np(array.dtype), kind="ExternalInput").ap()
    out = nc.dram_tensor("out_0", (1, T, D), F32, kind="ExternalOutput").ap()
    network(nc, args, out)
    r = _run(nc, [arrays], core_ids=[0])
    return _np.asarray(r.results[0]["out_0"])
```
